# Optimizing a Trainium2 kernel written in Bass

```python
import numpy as np
import jax
import jax.numpy as jnp

def _softmax(x, axis=-1):
    return jax.nn.softmax(x, axis=axis)
def _gelu(x):
    return jax.nn.gelu(x, approximate=True)
def _silu(x):
    return jax.nn.silu(x)
def _sigmoid(x):
    return jax.nn.sigmoid(x)
def _layernorm(x, axis=-1, eps=1e-5):
    m = jnp.mean(x, axis=axis, keepdims=True)
    v = jnp.var(x, axis=axis, keepdims=True)
    return (x - m) / jnp.sqrt(v + eps)
def _scatter_add(tgt, idx, src, axis=0):
    return tgt.at[idx].add(src)
def _segment_sum(src, seg, n):
    return jax.ops.segment_sum(src, seg, n)

kernel_name = 'mk_conv_seq_d1_conv_nhwc64_566d78'

def setup_inputs(seed: int = 0):
    np.random.seed(seed)
    _w = jnp.asarray
    def _rec_inputs():
        import jax
        import jax.numpy as jnp
        _gk = jax.random.key(seed)
        x = 7.22e-05 + 1 * jax.random.normal(jax.random.fold_in(_gk, 1), (8, 128, 128, 64), jnp.float32)
        return x
    x = _rec_inputs()
    def _L0_conv_setup():
        import jax, jax.numpy as jnp
        import numpy as np
        KR = 3

        def _neighborhood(x):
            B, H, W, C = x.shape
            xp = jnp.pad(x, ((0, 0), (1, 1), (1, 1), (0, 0)))
            views = [xp[:, 1 + i:1 + i + H, 1 + j:1 + j + W, :] for i in (-1, 0, 1) for j in (-1, 0, 1)]
            return jnp.stack(views, axis=3)

        def _conv(x, w, b):
            return jax.lax.conv_general_dilated(x, w, window_strides=(1, 1), padding='SAME', dimension_numbers=('NHWC', 'HWIO', 'NHWC')) + b
        key = jax.random.key(seed)
        ks = jax.random.split(key, 10)
        B, H, W, D = (8, 128, 128, 64)
        g = lambda k, shape, fan: jax.random.normal(k, shape, jnp.float32) * np.float32(1.0 / np.sqrt(fan))
        return {'x': jax.random.normal(ks[0], (B, H, W, D), jnp.float32), 'Q_P': g(ks[1], (D, D), D), 'K_P': g(ks[2], (D, D), D), 'V_P': g(ks[3], (D, D), D), 'ff1_kernel': g(ks[4], (3, 3, D, D), 9 * D), 'ff1_bias': jax.random.normal(ks[5], (D,), jnp.float32) * 0.01, 'ff2_kernel': g(ks[6], (3, 3, D, 2 * D), 9 * D), 'ff2_bias': jax.random.normal(ks[7], (2 * D,), jnp.float32) * 0.01, 'ff3_kernel': g(ks[8], (3, 3, 2 * D, D), 9 * 2 * D), 'ff3_bias': jax.random.normal(ks[9], (D,), jnp.float32) * 0.01}
    _L0_conv_all = _L0_conv_setup()
    _L0_conv_in = {k: v for k, v in _L0_conv_all.items() if k in ('Q_P', 'K_P', 'V_P', 'ff1_kernel', 'ff1_bias', 'ff2_kernel', 'ff2_bias', 'ff3_kernel', 'ff3_bias', )}
    del _L0_conv_all

    return {
        "x": x,
        "L0_conv_Q_P": _L0_conv_in["Q_P"],
        "L0_conv_K_P": _L0_conv_in["K_P"],
        "L0_conv_V_P": _L0_conv_in["V_P"],
        "L0_conv_ff1_kernel": _L0_conv_in["ff1_kernel"],
        "L0_conv_ff1_bias": _L0_conv_in["ff1_bias"],
        "L0_conv_ff2_kernel": _L0_conv_in["ff2_kernel"],
        "L0_conv_ff2_bias": _L0_conv_in["ff2_bias"],
        "L0_conv_ff3_kernel": _L0_conv_in["ff3_kernel"],
        "L0_conv_ff3_bias": _L0_conv_in["ff3_bias"],
    }

def reference(x, L0_conv_Q_P, L0_conv_K_P, L0_conv_V_P, L0_conv_ff1_kernel, L0_conv_ff1_bias, L0_conv_ff2_kernel, L0_conv_ff2_bias, L0_conv_ff3_kernel, L0_conv_ff3_bias):
    import jax
    import jax.numpy as jnp
    def _L0_conv_ref(x, Q_P, K_P, V_P, ff1_kernel, ff1_bias, ff2_kernel, ff2_bias, ff3_kernel, ff3_bias):
        import jax, jax.numpy as jnp
        import numpy as np
        KR = 3

        def _neighborhood(x):
            B, H, W, C = x.shape
            xp = jnp.pad(x, ((0, 0), (1, 1), (1, 1), (0, 0)))
            views = [xp[:, 1 + i:1 + i + H, 1 + j:1 + j + W, :] for i in (-1, 0, 1) for j in (-1, 0, 1)]
            return jnp.stack(views, axis=3)

        def _conv(x, w, b):
            return jax.lax.conv_general_dilated(x, w, window_strides=(1, 1), padding='SAME', dimension_numbers=('NHWC', 'HWIO', 'NHWC')) + b
        B, H, W, D = x.shape
        stk = _neighborhood(x)
        mask = _neighborhood(jnp.ones((B, H, W, 1), x.dtype))
        mask = mask[..., 0]
        q = jnp.einsum('bhwd,de->bhwe', x, Q_P)
        k = jnp.einsum('bhwkd,de->bhwke', stk, K_P)
        v = jnp.einsum('bhwkd,de->bhwke', stk, V_P)
        scores = jnp.einsum('bhwke,bhwe->bhwk', k, q) * mask
        alpha = jax.nn.softmax(scores, axis=-1)
        attn = jnp.einsum('bhwk,bhwke->bhwe', alpha, v)
        t = x + attn
        t_in = t
        t = jax.nn.relu(_conv(t, ff1_kernel, ff1_bias))
        t = jax.nn.relu(_conv(t, ff2_kernel, ff2_bias))
        t = jax.nn.relu(_conv(t, ff3_kernel, ff3_bias))
        return t_in + t

    def _gn(v, G=32, eps=1e-5):
        B_, H_, W_, C_ = v.shape
        g = v.reshape(B_, H_, W_, G, C_ // G)
        m = jnp.mean(g, axis=(1, 2, 4), keepdims=True)
        s = jnp.var(g, axis=(1, 2, 4), keepdims=True)
        return ((g - m) / jnp.sqrt(s + eps)).reshape(v.shape)

    def _ln_c(v, eps=1e-6):
        m = jnp.mean(v, axis=-1, keepdims=True)
        s = jnp.var(v, axis=-1, keepdims=True)
        return (v - m) / jnp.sqrt(s + eps)

    def _ln_t(v, eps=1e-5):
        m = jnp.mean(v, axis=-1, keepdims=True)
        s = jnp.var(v, axis=-1, keepdims=True)
        return (v - m) / jnp.sqrt(s + eps)

    def _to_tokens(v):
        B_, H_, W_, C_ = v.shape
        return v.reshape(B_, H_ * W_, C_)
    def _from_tokens(t, like):
        return t.reshape(like.shape)

    x = _L0_conv_ref(x, L0_conv_Q_P, L0_conv_K_P, L0_conv_V_P, L0_conv_ff1_kernel, L0_conv_ff1_bias, L0_conv_ff2_kernel, L0_conv_ff2_bias, L0_conv_ff3_kernel, L0_conv_ff3_bias)
    return x


_drawn_inputs = setup_inputs


def setup_inputs(seed=0):
    import zlib

    import numpy as np

    out = dict(_drawn_inputs(seed))
    spreads = {}
    factors = {'L0_conv_ff1_bias': 21.716, 'L0_conv_ff2_bias': 8.0, 'L0_conv_ff3_bias': 8.0}
    for name, (base, spread) in spreads.items():
        noise = np.random.default_rng([zlib.crc32(name.encode()), seed]).standard_normal(out[name].shape)
        drawn = base * np.exp(spread * noise) if base else spread * noise
        out[name] = jnp.asarray(drawn.astype(out[name].dtype))
    for name, factor in factors.items():
        out[name] = (out[name] * factor).astype(out[name].dtype)
    return out
```

```python
from contextlib import ExitStack

import concourse.bass as bass
from concourse import mybir
import numpy as np

F32 = mybir.dt.float32
F32R = mybir.dt.float32r
BF16 = mybir.dt.bfloat16
ALU = mybir.AluOpType
ACT = mybir.ActivationFunctionType
AX_X = mybir.AxisListType.X

IMAGES, H, W, C = 8, 128, 128, 64
PAIRS = IMAGES // 2
BAND = 8
BANDS = H // BAND
STEPS = BANDS + 1
PATCH = 8
HALO = PATCH + 2
KEYS = HALO * HALO
PATCHES = W // PATCH
GROUP = 4
GROUPS = PATCHES // GROUP
HALF = PATCHES // 2
WP = W + 2
RP = BAND // 2
LOADS = PAIRS * BANDS + 3
NEG = -3.0e38
TILES = 8
SPLITS = 6


def build(nc, x_bands, x_keys, qt2, kt, vbd, w1, w2, w3, b1, b2, b3, window, eye, eye16, out):
    with ExitStack() as ctx:
        def sb(name, shape, dt):
            return ctx.enter_context(nc.sbuf_tensor(name, shape, dt))

        def pb(name, shape):
            return ctx.enter_context(nc.psum_tensor(name, shape, F32))

        def sem(name):
            return ctx.enter_context(nc.semaphore(name))

        qt_sb = sb("qt_sb", [C, 128], F32)
        kt_sb = sb("kt_sb", [C, C], F32)
        qk = sb("qk", [128, 128], F32)
        v_sb = sb("v_sb", [128, 128], F32)
        w_raw = [sb(f"w{i + 1}_raw", [128, n, 128], F32) for i, n in enumerate((6, 12, 12))]
        w1h = sb("w1h", [128, 6, 128], F32R)
        w1l = sb("w1l", [128, 6, 128], F32R)
        w2h = sb("w2h", [128, 12, 128], F32R)
        w2l = sb("w2l", [128, 12, 128], F32R)
        w3h = sb("w3h", [128, 12, 128], F32R)
        w3l = sb("w3l", [128, 12, 128], F32R)
        bias = sb("bias", [128, 3], F32)
        window_sb = sb("window_sb", [128, KEYS], BF16)
        eye_sb = sb("eye_sb", [128, 128], F32)
        eye16_sb = sb("eye16_sb", [128, 128], BF16)
        xc = sb("xc", [128, 2, HALO, WP], F32)
        xk = sb("xk", [KEYS, 2, PATCHES, 128], F32)
        rbd = sb("rbd", [128, 2, PATCHES, 2, C], F32)
        negmax = sb("negmax", [128, 2, GROUP], F32)
        expsum = sb("expsum", [128, 2, GROUP], F32)
        expinv = sb("expinv", [128, 2, GROUP], F32)
        prob = sb("prob", [128, 2, GROUP, KEYS], F32)
        probt = sb("probt", [KEYS, 2, GROUP, 128], F32)
        y = sb("y", [128, 2, HALF, C], F32)
        tf = sb("tf", [128, 2, 2, RP + 2, W], F32)
        th = sb("th", [128, 2, RP + 1, WP], F32R)
        tl = sb("tl", [128, 2, RP + 1, WP], F32R)
        zeros = sb("zeros", [128, 4 * WP], F32)
        credits = sb("credits", [128, 8], F32)
        relu = sb("relu", [128, 2, RP, W], F32)
        uh = sb("uh", [128, 2, RP + 1, WP], F32R)
        ul = sb("ul", [128, 2, RP + 1, WP], F32R)
        vh = sb("vh", [128, 2, BAND + 3, WP], F32R)
        vl = sb("vl", [128, 2, BAND + 3, WP], F32R)
        z = sb("z", [128, 2, RP, W], F32)
        o_sb = sb("o_sb", [128, 2, RP, W], F32)

        conv_bank = [pb(f"conv_bank{i}", [128, RP, W]) for i in range(2)]
        score_bank = [pb(f"score_bank{i}", [128, 512]) for i in range(2)]
        turn_bank = [pb(f"turn_bank{i}", [128, GROUP, 128]) for i in range(2)]
        mix_bank = pb("mix_bank", [128, GROUP, 128])
        proj_bank = pb("proj_bank", [128, HALF, PATCH, PATCH])

        const_in = sem("const_in")
        w_in = [sem(f"w{i}_in") for i in (1, 2, 3)]
        w_high = sem("w_high")
        w_split = sem("w_split")
        zeroed = sem("zeroed")
        qk_done = sem("qk_done")
        qk_ready = sem("qk_ready")
        xc_in = [sem(f"xc{i}_in") for i in range(2)]
        xk_in = [sem(f"xk{i}_in") for i in range(2)]
        proj_done = sem("proj_done")
        r_ready = sem("r_ready")
        scores_done = sem("scores_done")
        max_done = sem("max_done")
        exp_done = sem("exp_done")
        inv_done = sem("inv_done")
        prob_ready = sem("prob_ready")
        turned = sem("turned")
        probt_ready = sem("probt_ready")
        mixed = sem("mixed")
        y_ready = sem("y_ready")
        t_ready = sem("t_ready")
        th_ready = sem("th_ready")
        tl_ready = sem("tl_ready")
        t_halo = sem("t_halo")
        u_halo = sem("u_halo")
        v_halo = sem("v_halo")
        carried = sem("carried")
        tile_done = sem("tile_done")
        tile_read = sem("tile_read")
        low_ready = sem("low_ready")
        o_ready = sem("o_ready")
        sent = [sem(f"sent{i}") for i in range(2)]

        block = ctx.enter_context(nc.Block())

        def schedule(eng, step):
            with eng.Fori(0, PAIRS) as p:
                g0, b0, q0 = p * STEPS, p * BANDS, p * (BANDS // 2)
                step(g0, 0, b0 + 1, q0, 1, True)
                with eng.Fori(0, (BANDS - 2) // 2) as h:
                    for j in range(2):
                        step(g0 + h * 2 + (1 + j), 1 + j, b0 + h * 2 + (2 + j), q0 + h + 1, j, True)
                step(g0 + (BANDS - 1), BANDS - 1, b0 + BANDS, q0 + BANDS // 2, 0, False)
                step(g0 + BANDS, BANDS, b0 + BANDS, q0 + BANDS // 2, 0, True)

        def pairs1(k):
            if k == 0:
                return [(slice(0, 128), 1, RP), (slice(C, 128), 0, 1)]
            return [(slice(0, C), 0, 1)] if k == BANDS else [(slice(0, 128), 0, RP)]

        def pairs2(k):
            return (1, RP) if k == 0 else (0, 1) if k == BANDS else (0, RP)

        def pairs3(k):
            return (2, RP) if k == 0 else (0, 2) if k == BANDS else (0, RP)

        def v_rows(t, i, even, lo, hi):
            first = 4 - even
            return t[:, i, first + 2 * lo:first + 2 * hi - 1:2, 1:1 + W]

        @block.sync
        def _(sp):
            for dst, src in ((qt_sb, qt2), (kt_sb, kt), (v_sb, vbd), (window_sb, window), (eye_sb, eye),
                             (eye16_sb, eye16)):
                sp.dma_start(dst[:], src).then_inc(const_in, 16)
            for i, src in enumerate((b1, b2, b3)):
                sp.dma_start(bias[:, i:i + 1], src).then_inc(const_in, 16)

            def load_xc(b, par):
                sp.dma_start(xc[:, par], x_bands[b]).then_inc(xc_in[par], 16)

            def load_xk(b, par):
                sp.dma_start(xk[:, par], x_keys[b]).then_inc(xk_in[par], 16)

            load_xc(0, 0)
            load_xk(0, 0)
            load_xc(1, 1)
            for i, src in enumerate((w1, w2, w3)):
                sp.dma_start(w_raw[i][:], src).then_inc(w_in[i], 16)
            load_xk(1, 1)
            sp.wait_ge(mixed, GROUPS)
            load_xk(2, 0)
            sp.wait_ge(t_ready, 2)
            load_xc(2, 0)

            def step(G, k, b, q, par, att):
                if att:
                    sp.wait_ge(mixed, b * GROUPS + GROUPS)
                    load_xk(b + 2, par)
                lo, hi = pairs3(k)
                for i in range(2):
                    if att and i == 1:
                        sp.wait_ge(t_ready, b * 2 + 2)
                        load_xc(b + 2, par)
                    sp.wait_ge(o_ready, G * 2 + (i + 3))
                    sp.dma_start(out[i, :, G, lo:hi], o_sb[:, i, lo:hi]).then_inc(sent[i], 16)

            schedule(sp, step)
            for i in range(2):
                sp.wait_ge(sent[i], 16 * (PAIRS * STEPS + 1))
                sp.wait_ge(xc_in[i], 16 * ((LOADS + 1 - i) // 2))
                sp.wait_ge(xk_in[i], 16 * ((LOADS + 1 - i) // 2))

        @block.tensor
        def _(pe):
            def proj(weights, moving):
                nc.tensor.matmul(proj_bank[:], weights, moving, start=True, stop=True).then_inc(proj_done, 1)

            def r_product(b, par, half):
                if not isinstance(b, int):
                    pe.wait_ge(t_ready, b * 2 - (1 - half))
                elif b:
                    pe.wait_ge(t_ready, b * 2 - (1 - half))
                elif half:
                    pe.wait_ge(r_ready, 1)
                band = xc[:, par, 1:1 + BAND, 1 + half * 64:65 + half * 64]
                proj(qk[:], band.rearrange("c r (a s) -> c a r s", s=PATCH))

            def v_product(b, half):
                pe.wait_ge(y_ready, b * GROUPS + 2 * (half + 1))
                pe.wait_ge(r_ready, b * 2 + (half + 2))
                proj(v_sb[:], y[:, half])

            def scores(b, par, g):
                pe.wait_ge(r_ready, b * 2 + (g // 2 + 1))
                if not (isinstance(b, int) and g < 2):
                    pe.wait_ge(exp_done, b * GROUPS + (g - 1))
                bank = score_bank[g % 2][:, 0:GROUP * KEYS].rearrange("q (a n) -> q a n", n=KEYS)
                nc.tensor.matmul(bank, eye16_sb[:],
                                 window_sb[:].rearrange("q (o n) -> q o n", o=1).broadcast_to([128, GROUP, KEYS]),
                                 start=True, stop=False)
                for a in range(GROUP):
                    patch = g * GROUP + a
                    last = nc.tensor.matmul(bank[:, a], rbd[:, par, patch],
                                            xc[:, par, :, patch * PATCH:patch * PATCH + HALO],
                                            start=False, stop=a == GROUP - 1)
                last.then_inc(scores_done, 1)

            def turn(b, g):
                pe.wait_ge(prob_ready, b * GROUPS + (g + 1))
                if not (isinstance(b, int) and g < 2):
                    pe.wait_ge(probt_ready, b * GROUPS + (g - 1))
                for a in range(GROUP):
                    last = nc.tensor.transpose(turn_bank[g % 2][0:KEYS, a], prob[:, g % 2, a], eye_sb[:])
                last.then_inc(turned, 1)

            def mix(b, q, par, g):
                if g == 0:
                    pe.wait_ge(xk_in[par], q * 16 + 16)
                pe.wait_ge(probt_ready, b * GROUPS + (g + 1))
                if not (isinstance(b, int) and g == 0):
                    pe.wait_ge(y_ready, b * GROUPS + g)
                for a in range(GROUP):
                    last = nc.tensor.matmul(mix_bank[:, a], xk[:, par, g * GROUP + a], probt[:, g % 2, a],
                                            start=True, stop=True)
                last.then_inc(mixed, 1)

            def accumulate(G, j, products, part=0, of=1):
                lo, hi = products[0][2], products[0][3]
                if part == 0:
                    pe.wait_ge(tile_read, G * TILES + (j + 1))
                n = len(products)
                for i in range(n * part // of, n * (part + 1) // of):
                    weights, moving, _, _ = products[i]
                    last = nc.tensor.matmul(conv_bank[j % 2][:, lo:hi], weights, moving,
                                            start=i == 0, stop=i == n - 1)
                if part == of - 1:
                    last.then_inc(tile_done, 1)

            def passes(taps, wh, wl, xh, xl, lo, hi):
                found = []
                for weights, data in ((wh, xh), (wh, xl), (wl, xh)):
                    for n, rows, col in taps:
                        found.append((weights[:, n], data(rows, col), lo, hi))
                return found

            def conv1(i, lo, hi):
                taps = [(s * 3 + c, s, c) for s in range(2) for c in range(3)]
                at = lambda t: lambda s, c: t[:, i, lo + s:hi + s, c:c + W]
                return passes(taps, w1h, w1l, at(th), at(tl), lo, hi)

            def conv2(i, even, lo, hi):
                taps = [((2 * even + s) * 3 + c, s, c) for s in range(2) for c in range(3)]
                at = lambda t: lambda s, c: t[:, i, lo + s:hi + s, c:c + W]
                return passes(taps, w2h, w2l, at(uh), at(ul), lo, hi)

            def conv3(i, lo, hi):
                taps = [(s * 3 + c, s, c) for s in range(4) for c in range(3)]
                at = lambda t: lambda s, c: t[:, i, 2 * lo + s:2 * hi + s - 1:2, c:c + W]
                return passes(taps, w3h, w3l, at(vh), at(vl), lo, hi)

            pe.wait_ge(const_in, 16 * 9)
            nc.tensor.matmul(score_bank[0][:, 0:C], qt_sb[:], kt_sb[:], start=True, stop=True).then_inc(qk_done, 1)
            pe.wait_ge(qk_ready, 1)
            pe.wait_ge(xc_in[0], 16)
            for half in range(2):
                r_product(0, 0, half)
            scores(0, 0, 0)
            scores(0, 0, 1)
            turn(0, 0)
            scores(0, 0, 2)
            turn(0, 1)
            mix(0, 0, 0, 0)
            scores(0, 0, 3)
            turn(0, 2)
            mix(0, 0, 0, 1)
            v_product(0, 0)
            turn(0, 3)
            mix(0, 0, 0, 2)
            pe.wait_ge(xc_in[1], 16)
            r_product(1, 1, 0)
            mix(0, 0, 0, 3)
            v_product(0, 1)
            r_product(1, 1, 1)
            pe.wait_ge(w_split, 3)

            def step(G, k, b, q, par, att):
                lo, hi = (0, 1) if k == BANDS else (0, RP)
                pe.wait_ge(tl_ready, b * 2)
                pe.wait_ge(t_halo, G + 1)
                accumulate(G, 0, conv1(0, lo, hi))
                if att:
                    scores(b, par, 0)
                accumulate(G, 1, conv1(1, lo, hi))
                if att:
                    scores(b, par, 1)
                    turn(b, 0)
                pe.wait_ge(low_ready, G * SPLITS + 3)
                accumulate(G, 2, conv2(0, 0, *pairs2(k)))
                if att:
                    scores(b, par, 2)
                    turn(b, 1)
                    mix(b, q, par, 0)
                accumulate(G, 3, conv2(0, 1, *pairs2(k)))
                if att:
                    scores(b, par, 3)
                    turn(b, 2)
                    mix(b, q, par, 1)
                pe.wait_ge(low_ready, G * SPLITS + 4)
                accumulate(G, 4, conv2(1, 0, *pairs2(k)))
                if att:
                    v_product(b, 0)
                    turn(b, 3)
                    mix(b, q, par, 2)
                accumulate(G, 5, conv2(1, 1, *pairs2(k)))
                if att:
                    pe.wait_ge(xc_in[1 - par], (q + (1 + par)) * 16)
                    r_product(b + 1, 1 - par, 0)
                    mix(b, q, par, 3)
                pe.wait_ge(low_ready, G * SPLITS + 6)
                accumulate(G, 6, conv3(0, *pairs3(k)))
                if att:
                    v_product(b, 1)
                pe.wait_ge(low_ready, G * SPLITS + 8)
                accumulate(G, 7, conv3(1, *pairs3(k)), 0, 2)
                if att:
                    r_product(b + 1, 1 - par, 1)
                accumulate(G, 7, conv3(1, *pairs3(k)), 1, 2)

            schedule(pe, step)

        @block.scalar
        def _(act):
            def exps(b, g):
                act.wait_ge(max_done, b * GROUPS + (g + 1))
                for a in range(GROUP):
                    last = nc.scalar.activation(prob[:, g % 2, a], score_bank[g % 2][:, a * KEYS:(a + 1) * KEYS],
                                                ACT.Exp, bias=negmax[:, g % 2, a:a + 1],
                                                accum_out=expsum[:, g % 2, a:a + 1])
                last.then_inc(exp_done, 1)

            def keep_y(b, g):
                act.wait_ge(mixed, b * GROUPS + (g + 1))
                half, a = g // 2, (g % 2) * GROUP
                nc.scalar.copy(y[0:C, half, a:a + GROUP], mix_bank[0:C, :, 0:C])
                nc.scalar.copy(y[C:128, half, a:a + GROUP], mix_bank[C:128, :, C:128]).then_inc(y_ready, 1)

            def t_high(G, b, par, half):
                act.wait_ge(t_ready, b * 2 + (half + 1))
                if half == 0 and G is not None:
                    act.wait_ge(t_halo, G + 2)
                nc.scalar.copy(th[:, :, 1:RP + 1, 1 + 64 * half:65 + 64 * half],
                               tf[:, par, :, 2:RP + 2, 64 * half:64 * half + 64]).then_inc(th_ready, 1)

            def relu_twice(G, j, stage, regions, high):
                act.wait_ge(tile_done, G * TILES + (j + 1))
                act.wait_ge(low_ready, G * SPLITS + (j + 1))
                for parts, lo, hi in regions:
                    nc.scalar.activation(relu[parts, j % 2, lo:hi], conv_bank[j % 2][parts, lo:hi], ACT.Relu,
                                         bias=bias[parts, stage:stage + 1])
                for parts, lo, hi in regions:
                    last = nc.scalar.activation(high(parts, lo, hi), conv_bank[j % 2][parts, lo:hi], ACT.Relu,
                                                bias=bias[parts, stage:stage + 1])
                last.then_inc(tile_read, 1)

            def relu_last(G, i, lo, hi):
                act.wait_ge(tile_done, G * TILES + (7 + i))
                nc.scalar.activation(z[:, i, lo:hi], conv_bank[i][:, lo:hi], ACT.Relu,
                                     bias=bias[:, 2:3]).then_inc(tile_read, 1)

            act.wait_ge(const_in, 16 * 9)
            exps(0, 0)
            exps(0, 1)
            exps(0, 2)
            keep_y(0, 0)
            exps(0, 3)
            for g in range(1, 4):
                keep_y(0, g)
            act.wait_ge(zeroed, 1)
            for half in range(2):
                t_high(None, 0, 0, half)

            def step(G, k, b, q, par, att):
                def u(i):
                    act.wait_ge(u_halo, G * 2 + (i + 1))
                    relu_twice(G, i, 0, pairs1(k), lambda parts, lo, hi: uh[parts, i, 1 + lo:1 + hi, 1:1 + W])

                def v(i, even):
                    act.wait_ge(v_halo, G * 2 + (i + 1))
                    relu_twice(G, 2 + 2 * i + even, 1, [(slice(0, 128), *pairs2(k))],
                               lambda parts, lo, hi: v_rows(vh, i, even, lo, hi))

                u(0)
                if att:
                    exps(b, 0)
                u(1)
                if att:
                    exps(b, 1)
                v(0, 0)
                if att:
                    exps(b, 2)
                    keep_y(b, 0)
                v(0, 1)
                if att:
                    exps(b, 3)
                    keep_y(b, 1)
                v(1, 0)
                if att:
                    keep_y(b, 2)
                v(1, 1)
                if att:
                    keep_y(b, 3)
                    t_high(G, b, par, 0)
                relu_last(G, 0, *pairs3(k))
                if att:
                    t_high(G, b, par, 1)
                relu_last(G, 1, *pairs3(k))

            schedule(act, step)

        @block.vector
        def _(dve):
            def keep_r(par, half, use):
                dve.wait_ge(proj_done, use + 1)
                patches = slice(half * HALF, half * HALF + HALF)
                src = proj_bank[:].rearrange("c a r s -> c a (r s)")
                nc.vector.tensor_copy(rbd[0:C, par, patches, 0], src[0:C])
                nc.vector.tensor_copy(rbd[C:128, par, patches, 1], src[C:128]).then_inc(r_ready, 1)

            def max_scores(b, g):
                dve.wait_ge(scores_done, b * GROUPS + (g + 1))
                nc.vector.tensor_reduce(negmax[:, g % 2],
                                        score_bank[g % 2][:, 0:GROUP * KEYS].rearrange("q (a n) -> q a n", n=KEYS),
                                        AX_X, ALU.max, negate=True).then_inc(max_done, 1)

            def norm(b, g):
                dve.wait_ge(exp_done, b * GROUPS + (g + 1))
                nc.vector.reciprocal(expinv[:, g % 2], expsum[:, g % 2]).then_inc(inv_done, 1)
                dve.wait_ge(inv_done, b * GROUPS + (g + 1))
                inv = expinv[:, g % 2].rearrange("q (a o) -> q a o", o=1).broadcast_to([128, GROUP, KEYS])
                nc.vector.tensor_tensor(prob[:, g % 2], prob[:, g % 2], inv, ALU.mult).then_inc(prob_ready, 1)

            def keep_turned(b, g):
                dve.wait_ge(turned, b * GROUPS + (g + 1))
                nc.vector.tensor_copy(probt[:, g % 2], turn_bank[g % 2][0:KEYS]).then_inc(probt_ready, 1)

            def add_x(G, b, par, half, use):
                dve.wait_ge(proj_done, use + 1)
                if half == 0 and G is not None:
                    dve.wait_ge(carried, G + 1)
                for i in range(2):
                    src = slice(i * C, i * C + C)
                    for odd in range(2):
                        o = tf[odd * C:odd * C + C, par, i, 2:RP + 2, 64 * half:64 * half + 64]
                        a = proj_bank[src, :, odd::2, :].rearrange("c a r s -> c r a s")
                        x = xc[src, par, 1 + odd:1 + BAND:2, 1 + 64 * half:65 + 64 * half]
                        last = nc.vector.tensor_tensor(o.rearrange("c r (a s) -> c r a s", s=PATCH), a,
                                                       x.rearrange("c r (a s) -> c r a s", s=PATCH), ALU.add)
                last.then_inc(t_ready, 1)

            def t_low(b, par, half):
                dve.wait_ge(th_ready, b * 2 + (half + 1))
                cols = slice(1 + 64 * half, 65 + 64 * half)
                nc.vector.tensor_tensor(tl[:, :, 1:RP + 1, cols],
                                        tf[:, par, :, 2:RP + 2, 64 * half:64 * half + 64],
                                        th[:, :, 1:RP + 1, cols].bitcast(F32), ALU.subtract).then_inc(tl_ready, 1)

            for t in (th, tl, uh, ul, vh, vl):
                nc.vector.memset(t[:].bitcast(F32), 0.0)
            nc.vector.memset(zeros[:], 0.0)
            nc.vector.memset(tf[:], 0.0)
            nc.vector.memset(rbd[:], 0.0)
            nc.vector.memset(qk[:], 0.0).then_inc(zeroed, 1)
            dve.wait_ge(zeroed, 1)
            dve.wait_ge(qk_done, 1)
            nc.vector.tensor_copy(qk[0:C, 0:C], score_bank[0][0:C, 0:C])
            nc.vector.tensor_copy(qk[C:128, C:128], score_bank[0][C:128, 0:C]).then_inc(qk_ready, 1)
            for half in range(2):
                keep_r(0, half, half)
            def split(i, high, low):
                dve.wait_ge(w_in[i], 16)
                nc.vector.tensor_copy(high[:], w_raw[i][:]).then_inc(w_high, 1)
                dve.wait_ge(w_high, i + 1)
                nc.vector.tensor_tensor(low[:], w_raw[i][:], high[:].bitcast(F32), ALU.subtract).then_inc(w_split, 1)

            max_scores(0, 0)
            max_scores(0, 1)
            norm(0, 0)
            keep_turned(0, 0)
            norm(0, 1)
            max_scores(0, 2)
            keep_turned(0, 1)
            norm(0, 2)
            max_scores(0, 3)
            keep_turned(0, 2)
            norm(0, 3)
            keep_turned(0, 3)
            add_x(None, 0, 0, 0, 2)
            keep_r(1, 0, 3)
            add_x(None, 0, 0, 1, 4)
            keep_r(1, 1, 5)
            for half in range(2):
                t_low(0, 0, half)
            for i, (high, low) in enumerate(((w1h, w1l), (w2h, w2l), (w3h, w3l))):
                split(i, high, low)

            def step(G, k, b, q, par, att):
                def low(j, regions, high_part, low_part):
                    dve.wait_ge(tile_read, G * TILES + (j + 3))
                    for region in regions:
                        parts, lo, hi = region
                        last = nc.vector.tensor_tensor(low_part(*region), relu[parts, j % 2, lo:hi],
                                                       high_part(*region).bitcast(F32), ALU.subtract)
                    last.then_inc(low_ready, 1)

                def u(i):
                    at = lambda t: lambda parts, lo, hi: t[parts, i, 1 + lo:1 + hi, 1:1 + W]
                    low(i, pairs1(k), at(uh), at(ul))

                def v(i, even):
                    at = lambda t: lambda parts, lo, hi: v_rows(t, i, even, lo, hi)
                    low(2 + 2 * i + even, [(slice(0, 128), *pairs2(k))], at(vh), at(vl))

                def finish(i):
                    lo, hi = pairs3(k)
                    dve.wait_ge(tile_read, G * TILES + (9 + i))
                    dve.wait_ge(carried, G + 1)
                    dve.wait_ge(sent[i], G * 16 + 16)
                    nc.vector.tensor_tensor(o_sb[:, i, lo:hi], z[:, i, lo:hi], tf[:, k % 2, i, lo:hi],
                                            ALU.add).then_inc(o_ready, 1)

                u(0)
                if att:
                    max_scores(b, 0)
                    norm(b, 0)
                u(1)
                if att:
                    max_scores(b, 1)
                    keep_turned(b, 0)
                    norm(b, 1)
                v(0, 0)
                if att:
                    max_scores(b, 2)
                    keep_turned(b, 1)
                    norm(b, 2)
                v(0, 1)
                if att:
                    max_scores(b, 3)
                    keep_turned(b, 2)
                    norm(b, 3)
                v(1, 0)
                if att:
                    add_x(G, b, par, 0, b * 4 + 2)
                    keep_turned(b, 3)
                v(1, 1)
                if att:
                    keep_r(1 - par, 0, b * 4 + 3)
                    t_low(b, par, 0)
                finish(0)
                if att:
                    add_x(G, b, par, 1, b * 4 + 4)
                    t_low(b, par, 1)
                    keep_r(1 - par, 1, b * 4 + 5)
                finish(1)

            schedule(dve, step)

        @block.gpsimd
        def _(pool):
            def zero(tile):
                return nc.gpsimd.memset(tile.bitcast(F32), 0.0)

            def copy(dst, src):
                none = zeros[:, 0:int(np.prod(dst.shape[1:]))]
                if len(dst.shape) == 3:
                    none = none.rearrange("c (a b) -> c a b", a=dst.shape[1])
                if len(dst.shape) == 4:
                    none = none.rearrange("c (i a b) -> c i a b", i=dst.shape[1], a=dst.shape[2])
                return nc.gpsimd.tensor_tensor(dst, src, none, ALU.add)

            pool.wait_ge(zeroed, 1)
            for i, (credit, n) in enumerate(((t_halo, 1), (u_halo, 2), (v_halo, 2), (tile_read, 2),
                                             (low_ready, 2), (o_ready, 2), (sent[0], 16), (sent[1], 16))):
                zero(credits[:, i:i + 1]).then_inc(credit, n)

            def step(G, k, b, q, par, att):
                pool.wait_ge(o_ready, G * 2 + 2)
                pool.wait_ge(t_ready, b * 2)
                copy(tf[:, k % 2, :, 0:2], tf[:, 1 - k % 2, :, RP:RP + 2]).then_inc(carried, 1)
                pool.wait_ge(tile_done, G * TILES + 2)
                for t in (th, tl):
                    if k == BANDS:
                        last = copy(t[:, :, 0], zeros[:, 0:2 * WP].rearrange("c (i w) -> c i w", i=2))
                    else:
                        last = copy(t[:, :, 0], t[:, :, RP])
                    if k == BANDS - 1:
                        last = zero(t[:, :, 1])
                last.then_inc(t_halo, 1)
                for i in range(2):
                    pool.wait_ge(tile_done, G * TILES + (4 + 2 * i))
                    for t in (uh, ul):
                        last = copy(t[:, i, 0], t[:, i, RP])
                        if k >= BANDS - 1:
                            last = zero(t[:, i, 1])
                    last.then_inc(u_halo, 1)
                for i in range(2):
                    pool.wait_ge(tile_done, G * TILES + (7 + i))
                    for t in (vh, vl):
                        last = copy(t[:, i, 0:3], t[:, i, BAND:BAND + 3])
                        if k == BANDS:
                            last = zero(t[:, i, 4])
                        if k == BANDS - 1:
                            last = zero(t[:, i, 5])
                    last.then_inc(v_halo, 1)

            schedule(pool, step)


def kernel(**inputs):
    import concourse.bacc as bacc
    from concourse.bass_utils import run_bass_kernel_spmd

    given = {n.removeprefix("L0_conv_"): np.asarray(a) for n, a in inputs.items()}
    f32 = np.float32

    padded = np.zeros((PAIRS, 2, H + 2, WP, C), f32)
    padded[:, :, 1:-1, 1:-1] = given["x"].reshape(2, PAIRS, H, W, C).swapaxes(0, 1)
    x_bands = np.zeros((LOADS, 128, HALO, WP), f32)
    x_keys = np.zeros((LOADS, HALO, HALO, PATCHES, 2, C), f32)
    for n in range(PAIRS * BANDS):
        p, row = n // BANDS, n % BANDS * BAND
        band = padded[p, :, row:row + HALO]
        x_bands[n] = band.transpose(0, 3, 1, 2).reshape(128, HALO, WP)
        for a in range(PATCHES):
            x_keys[n, :, :, a] = band[:, :, a * PATCH:a * PATCH + HALO].transpose(1, 2, 0, 3)

    vbd = np.zeros((128, 128), f32)
    vbd[:C, :C] = vbd[C:, C:] = given["V_P"]
    k1, k2, k3 = (given[f"ff{i}_kernel"] for i in (1, 2, 3))
    w1 = np.zeros((128, 2, 3, 128), f32)
    w2 = np.zeros((128, 4, 3, 128), f32)
    w3 = np.zeros((128, 4, 3, 128), f32)
    for c in range(3):
        for s in range(2):
            for i in range(2):
                for o in range(2):
                    tap = 2 * s + i - o
                    if 0 <= tap < 3:
                        w1[i * C:i * C + C, s, c, o * C:o * C + C] = k1[tap, c]
        for even in range(2):
            for s in range(2):
                for i in range(2):
                    tap = 2 * s + i - (0 if even else 1)
                    if 0 <= tap < 3:
                        w2[i * C:i * C + C, 2 * even + s, c] = k2[tap, c]
        for s in range(4):
            for o in range(2):
                if 0 <= s - o < 3:
                    w3[:, s, c, o * C:o * C + C] = k3[s - o, c]

    window = np.full((2, PATCH, PATCH, HALO, HALO), NEG, f32)
    for r in range(PATCH):
        for c in range(PATCH):
            window[:, r, c, r:r + 3, c:c + 3] = 0.0

    bf16 = mybir.dt.np(BF16)
    data = {
        "x_bands": x_bands,
        "x_keys": x_keys.reshape(LOADS, KEYS, PATCHES, 128),
        "qt2": np.concatenate([given["Q_P"].T, given["Q_P"].T], axis=1),
        "kt": given["K_P"].T,
        "vbd": vbd,
        "w1": w1.reshape(128, 6, 128),
        "w2": w2.reshape(128, 12, 128),
        "w3": w3.reshape(128, 12, 128),
        "b1": np.concatenate([given["ff1_bias"]] * 2).reshape(128, 1),
        "b2": given["ff2_bias"].reshape(128, 1),
        "b3": np.concatenate([given["ff3_bias"]] * 2).reshape(128, 1),
        "window": window.reshape(128, KEYS).astype(bf16),
        "eye": np.eye(128, dtype=f32),
        "eye16": np.eye(128, dtype=f32).astype(bf16),
    }
    nc = bacc.Bacc("TRN2", target_bir_lowering=False, num_devices=1)
    arrays, args = {}, []
    for name, a in data.items():
        arrays[name] = np.ascontiguousarray(a)
        args.append(nc.dram_tensor(name, a.shape, mybir.dt.from_np(a.dtype), kind="ExternalInput").ap())
    out = nc.dram_tensor("out", (2, 128, PAIRS * STEPS, RP, W), F32, kind="ExternalOutput").ap()
    build(nc, *args, out)
    got = run_bass_kernel_spmd(nc, [arrays], core_ids=[0]).results[0]["out"]
    got = got.reshape(2, 2, C, PAIRS, STEPS * RP, W)[:, :, :, :, 2:2 + H // 2]
    return np.ascontiguousarray(got.transpose(0, 3, 4, 1, 5, 2)).reshape(IMAGES, H, W, C)
```

```python
from contextlib import ExitStack

import concourse.bass as bass
from concourse import mybir
import numpy as np

F32 = mybir.dt.float32
F32R = mybir.dt.float32r
BF16 = mybir.dt.bfloat16
ALU = mybir.AluOpType
ACT = mybir.ActivationFunctionType
AX_X = mybir.AxisListType.X

IMAGES, H, W, C = 8, 128, 128, 64
PAIRS = IMAGES // 2
BAND = 8
BANDS = H // BAND
STEPS = BANDS + 1
ALL_STEPS = PAIRS * STEPS
PATCH = 8
HALO = PATCH + 2
KEYS = HALO * HALO
PATCHES = W // PATCH
GROUP = 4
GROUPS = PATCHES // GROUP
HALF = PATCHES // 2
WP = W + 2
WT = W // 2
RP = BAND // 2
LOADS = PAIRS * BANDS + 3
NEG = -3.0e38
FULL = slice(0, 128)

TILES = 14
STREAMS = (2, 1, 0, 3)
CONV3, ODD, EVEN = 0, 1, 2
BANK = (0, 1, 2, 0, 1, 2, 0, 1, 2, 0, 1, 2, 0, 1)
ACT_READS, DVE_READS = 5, 9
READ = {0: ("act", 1), 1: ("act", 2)}
for _set in range(3):
    READ[2 + 4 * _set] = ("act", 3 + _set)
    for _n in range(3):
        READ[3 + 4 * _set + _n] = ("dve", 3 * _set + _n + 1)


def first_tile(which):
    return 2 + 4 * which


def pairs2(k):
    return (1, RP) if k == 0 else (0, 1) if k == BANDS else (0, RP)


def pairs3(k):
    return (2, RP) if k == 1 else (0, 2) if k == 0 else (0, RP)


def build(nc, x_bands, x_keys, qt2, kt, vbd, w1, w2, w3, b1, b2, b3, window, eye, eye16, out):
    with ExitStack() as ctx:
        def sb(name, shape, dt):
            return ctx.enter_context(nc.sbuf_tensor(name, shape, dt))

        def pb(name, shape):
            return ctx.enter_context(nc.psum_tensor(name, shape, F32))

        def sem(name):
            return ctx.enter_context(nc.semaphore(name))

        qt_sb = sb("qt_sb", [C, 128], F32)
        kt_sb = sb("kt_sb", [C, C], F32)
        qk = sb("qk", [128, 128], F32)
        v_sb = sb("v_sb", [128, 128], F32)
        w1h = sb("w1h", [128, 6, 128], F32R)
        w1l = sb("w1l", [128, 6, 128], F32R)
        w2h = sb("w2h", [128, 4, 4, 128], F32R)
        w2l = sb("w2l", [128, 4, 4, 128], F32R)
        w3h = sb("w3h", [128, 4, 4, 128], F32R)
        w3l = sb("w3l", [128, 4, 4, 128], F32R)
        bias = sb("bias", [128, 3], F32)
        window_sb = sb("window_sb", [128, KEYS], BF16)
        eye_sb = sb("eye_sb", [128, 128], F32)
        eye16_sb = sb("eye16_sb", [128, 128], BF16)
        zeros = sb("zeros", [128, 1, 2, W], F32)
        credits = sb("credits", [128, 12], F32)
        xc = sb("xc", [128, 2, HALO, WP], F32)
        xk = sb("xk", [KEYS, PATCHES, 128], F32)
        rbd = sb("rbd", [128, PATCHES, 2, C], F32)
        negmax = sb("negmax", [128, 2, GROUP], F32)
        expsum = sb("expsum", [128, 2, GROUP], F32)
        expinv = sb("expinv", [128, 2, GROUP], F32)
        prob = sb("prob", [128, 2, GROUP, KEYS], F32)
        probt = sb("probt", [KEYS, 2, GROUP, 128], F32)
        y = sb("y", [128, 2, HALF, C], F32)
        tf = sb("tf", [128, 2, RP + 2, 2, W], F32)
        th = sb("th", [128, RP + 1, 2, WP], F32R)
        tl = sb("tl", [128, RP + 1, 2, WP], F32R)
        relued = sb("relued", [128, RP, 2, WP], F32)
        m2_sb = sb("m2_sb", [128, 2, RP, 2, WT], F32)
        work = sb("work", [128, 6 * RP * 2 * W], F32)
        size = RP * 2 * W
        d = [work[:, n * 2 * size:(n + 1) * 2 * size].rearrange("c (s m i w) -> c s m i w", s=RP, m=4, i=2)
             for n in (0, 1, 0)]
        sums = [work[:, n * size:(n + 1) * size].rearrange("c (s i w) -> c s i w", s=RP, i=2)
                for n in (4, 5, 5)]
        duh = sb("duh", [128, RP + 1, 4, 2, WT], F32R)
        dul = sb("dul", [128, RP + 1, 4, 2, WT], F32R)
        dvh = [sb(f"dvh{i}", [128, RP + 2 - i, 4, 2, WT], F32R) for i in range(2)]
        dvl = [sb(f"dvl{i}", [128, RP + 2 - i, 4, 2, WT], F32R) for i in range(2)]
        n1, n2 = 6 * 128, 12 * 128
        w1_raw = work[:, 0:n1].rearrange("c (m n) -> c m n", n=128)
        w2_raw = work[:, n1:n1 + n2].rearrange("c (s t n) -> c s t n", s=4, t=3)
        w3_raw = work[:, n1 + n2:n1 + 2 * n2].rearrange("c (s t n) -> c s t n", s=4, t=3)
        w_mid = work[:, n1 + 2 * n2:n1 + 2 * n2 + 1024].rearrange("c (m s n) -> c m s n", m=2, s=4)
        w_half = sb("w_half", [128, 4, 128], F32)

        conv_bank = [pb(f"conv_bank{i}", [128, 512]) for i in range(3)]
        score_bank = [pb(f"score_bank{i}", [128, 512]) for i in range(2)]
        turn_bank = pb("turn_bank", [128, GROUP, 128])
        mix_bank = pb("mix_bank", [128, GROUP, 128])
        proj_bank = pb("proj_bank", [128, HALF, PATCH, PATCH])

        const_in = sem("const_in")
        w_in = sem("w_in")
        w_stage = sem("w_stage")
        split_done = sem("split_done")
        zeroed = sem("zeroed")
        v_zeroed = sem("v_zeroed")
        qk_done = sem("qk_done")
        qk_ready = sem("qk_ready")
        xc_in = [sem(f"xc{i}_in") for i in range(2)]
        xk_in = sem("xk_in")
        proj_done = sem("proj_done")
        r_ready = sem("r_ready")
        scores_done = sem("scores_done")
        max_done = sem("max_done")
        exp_done = sem("exp_done")
        inv_done = sem("inv_done")
        prob_ready = sem("prob_ready")
        turned = sem("turned")
        probt_ready = sem("probt_ready")
        mixed = sem("mixed")
        y_ready = sem("y_ready")
        t_ready = sem("t_ready")
        th_ready = sem("th_ready")
        tl_ready = sem("tl_ready")
        tile_done = sem("tile_done")
        act_read = sem("act_read")
        dve_read = sem("dve_read")
        sum_done = sem("sum_done")
        relu_done = sem("relu_done")
        d_done = sem("d_done")
        high_done = sem("high_done")
        low_done = sem("low_done")
        out_ready = sem("out_ready")
        sent = sem("sent")
        t_kept = sem("t_kept")
        u_kept = sem("u_kept")
        v_kept = sem("v_kept")
        carried = sem("carried")

        block = ctx.enter_context(nc.Block())

        def schedule(eng, step):
            with eng.Fori(0, PAIRS) as p:
                g0, b0, q0 = p * STEPS, p * BANDS, p * (BANDS // 2)
                step(g0, 0, b0 + 1, q0, 1, True)
                step(g0 + 1, 1, b0 + 2, q0 + 1, 0, True)
                with eng.Fori(0, (BANDS - 4) // 2) as h:
                    for j in range(2):
                        step(g0 + h * 2 + (2 + j), 2 + j, b0 + h * 2 + (3 + j), q0 + h + (1 + j), 1 - j, True)
                step(g0 + (BANDS - 2), BANDS - 2, b0 + (BANDS - 1), q0 + (BANDS // 2 - 1), 1, True)
                step(g0 + (BANDS - 1), BANDS - 1, b0 + BANDS, q0 + BANDS // 2, 0, False)
                step(g0 + BANDS, BANDS, b0 + BANDS, q0 + BANDS // 2, 0, True)

        def tiles_done(G, tile):
            return G * TILES + (tile + 1 - (2 if G is ALL_STEPS else 0))

        def act_reads(G, n):
            return G * ACT_READS + (ACT_READS + n - (2 if G is ALL_STEPS else 0))

        def dve_reads(G, n):
            return G * DVE_READS + (DVE_READS + n)

        @block.sync
        def _(sp):
            for dst, src in ((qt_sb, qt2), (kt_sb, kt), (v_sb, vbd), (window_sb, window), (eye_sb, eye),
                             (eye16_sb, eye16)):
                sp.dma_start(dst[:], src).then_inc(const_in, 16)
            for i, src in enumerate((b1, b2, b3)):
                sp.dma_start(bias[:, i:i + 1], src).then_inc(const_in, 16)

            def move(t, to, at, n):
                return sp.dma_start(t[:, to:to + n].bitcast(F32), t[:, at:at + n].bitcast(F32))

            def load_xc(b, par):
                sp.dma_start(xc[:, par], x_bands[b]).then_inc(xc_in[par], 16)

            def load_xk(b):
                sp.dma_start(xk[:], x_keys[b]).then_inc(xk_in, 16)

            load_xc(0, 0)
            load_xk(0)
            load_xc(1, 1)
            for dst, src in ((w1_raw, w1), (w2_raw, w2), (w3_raw, w3)):
                sp.dma_start(dst, src).then_inc(w_in, 16)
            sp.wait_ge(mixed, GROUPS)
            load_xk(1)
            sp.wait_ge(t_ready, 2)
            load_xc(2, 0)

            def store(G, k):
                lo, hi = pairs3(k)
                sp.wait_ge(out_ready, G + 1)
                sp.dma_start(out[:, G, lo:hi], sums[CONV3][:, lo:hi]).then_inc(sent, 16)

            def step(G, k, b, q, par, att):
                if k:
                    if k < BANDS:
                        sp.wait_ge(t_ready, b * 2)
                    else:
                        sp.wait_ge(out_ready, G)
                    sp.dma_start(tf[:, k % 2, 0:2], tf[:, 1 - k % 2, RP:RP + 2]).then_inc(carried, 16)
                sp.wait_ge(tile_done, tiles_done(G, 1))
                for t in (th, tl):
                    move(t, 0, RP, 1).then_inc(t_kept, 16)
                sp.wait_ge(tile_done, tiles_done(G, 5))
                for t in (dvh, dvl):
                    move(t[0], 0, RP, 2).then_inc(v_kept, 16)
                    move(t[1], 0, RP, 1).then_inc(v_kept, 16)
                store(G, k)
                if att:
                    sp.wait_ge(mixed, b * GROUPS + GROUPS)
                    load_xk(b + 1)
                    sp.wait_ge(t_ready, b * 2 + 2)
                    load_xc(b + 2, par)
                sp.wait_ge(tile_done, tiles_done(G, 13))
                for t in (duh, dul):
                    move(t, 0, RP, 1).then_inc(u_kept, 16)

            schedule(sp, step)
            store(ALL_STEPS, 0)
            sp.wait_ge(sent, 16 * (ALL_STEPS + 2))
            sp.wait_ge(t_kept, 32 * (ALL_STEPS + 1))
            sp.wait_ge(u_kept, 32 * (ALL_STEPS + 1))
            sp.wait_ge(v_kept, 64 * ALL_STEPS)
            sp.wait_ge(carried, 16 * (PAIRS * BANDS + 1))
            sp.wait_ge(xk_in, 16 * (LOADS - 1))
            for i in range(2):
                sp.wait_ge(xc_in[i], 16 * ((LOADS + 1 - i) // 2))

        @block.tensor
        def _(pe):
            def proj(weights, moving):
                nc.tensor.matmul(proj_bank[:], weights, moving, start=True, stop=True).then_inc(proj_done, 1)

            def r_product(b, par, half):
                if not isinstance(b, int):
                    pe.wait_ge(t_ready, b * 2 - (1 - half))
                elif b:
                    pe.wait_ge(t_ready, b * 2 - (1 - half))
                elif half:
                    pe.wait_ge(r_ready, 1)
                band = xc[:, par, 1:1 + BAND, 1 + half * 64:65 + half * 64]
                proj(qk[:], band.rearrange("c r (a s) -> c a r s", s=PATCH))

            def v_product(b, half):
                pe.wait_ge(y_ready, b * GROUPS + 2 * (half + 1))
                pe.wait_ge(r_ready, b * 2 + (half + 2))
                proj(v_sb[:], y[:, half])

            def scores(b, par, g):
                pe.wait_ge(r_ready, b * 2 + (g // 2 + 1))
                if not (isinstance(b, int) and g < 2):
                    pe.wait_ge(exp_done, b * GROUPS + (g - 1))
                bank = score_bank[g % 2][:, 0:GROUP * KEYS].rearrange("q (a n) -> q a n", n=KEYS)
                nc.tensor.matmul(bank, eye16_sb[:],
                                 window_sb[:].rearrange("q (o n) -> q o n", o=1).broadcast_to([128, GROUP, KEYS]),
                                 start=True, stop=False)
                for a in range(GROUP):
                    patch = g * GROUP + a
                    last = nc.tensor.matmul(bank[:, a], rbd[:, patch],
                                            xc[:, par, :, patch * PATCH:patch * PATCH + HALO],
                                            start=False, stop=a == GROUP - 1)
                last.then_inc(scores_done, 1)

            def turn(b, g):
                pe.wait_ge(prob_ready, b * GROUPS + (g + 1))
                if not (isinstance(b, int) and g == 0):
                    pe.wait_ge(probt_ready, b * GROUPS + g)
                for a in range(GROUP):
                    last = nc.tensor.transpose(turn_bank[0:KEYS, a], prob[:, g % 2, a], eye_sb[:])
                last.then_inc(turned, 1)

            def mix(b, g):
                if g == 0:
                    pe.wait_ge(xk_in, b * 16 + 16)
                pe.wait_ge(probt_ready, b * GROUPS + (g + 1))
                if not (isinstance(b, int) and g == 0):
                    pe.wait_ge(y_ready, b * GROUPS + g)
                for a in range(GROUP):
                    last = nc.tensor.matmul(mix_bank[:, a], xk[:, g * GROUP + a], probt[:, g % 2, a],
                                            start=True, stop=True)
                last.then_inc(mixed, 1)

            def tile(G, n, products, low_ready=()):
                who, count = READ[n]
                before = [t for t in range(n) if BANK[t] == BANK[n]]
                if G is ALL_STEPS:
                    before = [t for t in before if t >= 2]
                if before:
                    who, count = READ[before[-1]]
                    pe.wait_ge(*(act_read, act_reads(G, count)) if who == "act" else (dve_read, dve_reads(G, count)))
                else:
                    who, count = READ[[t for t in range(TILES) if BANK[t] == BANK[n]][-1]]
                    if who == "act":
                        pe.wait_ge(act_read, G * ACT_READS + count)
                    else:
                        pe.wait_ge(dve_read, G * DVE_READS + count)
                for i, (weights, moving, lo, hi) in enumerate(products):
                    if low_ready and i == len(products) // 3 * 2:
                        pe.wait_ge(*low_ready)
                    last = nc.tensor.matmul(conv_bank[BANK[n]][:, lo * 128:hi * 128], weights, moving,
                                            start=i == 0, stop=i == len(products) - 1)
                last.then_inc(tile_done, 1)

            def passes(taps, wh, wl, xh, xl):
                return [(weights(n), data(lo, hi), lo, hi) for weights, part in ((wh, xh), (wl, xh), (wh, xl))
                        for n, data, lo, hi in ((n, part(s), lo, hi) for n, s, lo, hi in taps)]

            def conv1(k, i):
                taps = []
                if k < BANDS:
                    taps += [(3 + c, (1, c), 0, RP) for c in range(3)]
                taps += [(c, (0, c), 1 if k == 0 else 0, 1 if k == BANDS else RP) for c in range(3)]
                at = lambda t: lambda s: lambda lo, hi: t[:, lo + s[0]:hi + s[0], i, s[1]:s[1] + W]
                return passes(taps, lambda n: w1h[:, n], lambda n: w1l[:, n], at(th), at(tl))

            def conv2(k, even, m):
                at = lambda t: lambda s: lambda lo, hi: t[:, lo + s:hi + s, m]
                return passes([(2 * even + s, s, *pairs2(k)) for s in range(2)],
                              lambda n: w2h[:, m, n], lambda n: w2l[:, m, n], at(duh), at(dul))

            def conv3(k, m):
                at = lambda t: lambda s: lambda lo, hi: t[s % 2][:, lo + s // 2:hi + s // 2, m]
                return passes([(s, s, *pairs3(k)) for s in range(4)],
                              lambda n: w3h[:, m, n], lambda n: w3l[:, m, n], at(dvh), at(dvl))

            pe.wait_ge(const_in, 16 * 9)
            nc.tensor.matmul(score_bank[0][:, 0:C], qt_sb[:], kt_sb[:], start=True, stop=True).then_inc(qk_done, 1)
            pe.wait_ge(qk_ready, 1)
            pe.wait_ge(xc_in[0], 16)
            for half in range(2):
                r_product(0, 0, half)
            scores(0, 0, 0)
            scores(0, 0, 1)
            turn(0, 0)
            scores(0, 0, 2)
            turn(0, 1)
            mix(0, 0)
            scores(0, 0, 3)
            turn(0, 2)
            mix(0, 1)
            v_product(0, 0)
            turn(0, 3)
            mix(0, 2)
            pe.wait_ge(xc_in[1], 16)
            r_product(1, 1, 0)
            mix(0, 3)
            v_product(0, 1)
            r_product(1, 1, 1)
            pe.wait_ge(split_done, 1)
            pe.wait_ge(v_zeroed, 1)

            def step(G, k, b, q, par, att):
                def set_tile(which, n, low_ready=()):
                    m = STREAMS[n]
                    products = conv3(k, m) if which == CONV3 else conv2(k, which == EVEN, m)
                    tile(G, first_tile(which) + n, products, low_ready)

                pe.wait_ge(th_ready, b * 2)
                pe.wait_ge(t_kept, G * 32 + 32)
                tile(G, 0, conv1(k, 0), (tl_ready, b * 2))
                if att:
                    scores(b, par, 0)
                tile(G, 1, conv1(k, 1))
                if att:
                    scores(b, par, 1)
                pe.wait_ge(high_done, G * 3 + 3)
                set_tile(CONV3, 0, (low_done, G * 3 + 3))
                if att:
                    turn(b, 0)
                set_tile(CONV3, 1)
                if att:
                    scores(b, par, 2)
                    turn(b, 1)
                    mix(b, 0)
                set_tile(CONV3, 2)
                if att:
                    scores(b, par, 3)
                    turn(b, 2)
                    mix(b, 1)
                set_tile(CONV3, 3)
                if att:
                    turn(b, 3)
                    mix(b, 2)
                    v_product(b, 0)
                pe.wait_ge(high_done, G * 3 + 4)
                set_tile(ODD, 0, (low_done, G * 3 + 4))
                set_tile(ODD, 1)
                if att:
                    mix(b, 3)
                    pe.wait_ge(xc_in[1 - par], (q + (1 + par)) * 16)
                    r_product(b + 1, 1 - par, 0)
                set_tile(ODD, 2)
                set_tile(ODD, 3)
                if att:
                    v_product(b, 1)
                set_tile(EVEN, 0)
                set_tile(EVEN, 1)
                if att:
                    r_product(b + 1, 1 - par, 1)
                set_tile(EVEN, 2)
                set_tile(EVEN, 3)

            schedule(pe, step)
            pe.wait_ge(low_done, ALL_STEPS * 3 + 3)
            for n in range(4):
                tile(ALL_STEPS, first_tile(CONV3) + n, conv3(0, STREAMS[n]))

        @block.scalar
        def _(act):
            def exps(b, g):
                act.wait_ge(max_done, b * GROUPS + (g + 1))
                for a in range(GROUP):
                    last = nc.scalar.activation(prob[:, g % 2, a], score_bank[g % 2][:, a * KEYS:(a + 1) * KEYS],
                                                ACT.Exp, bias=negmax[:, g % 2, a:a + 1],
                                                accum_out=expsum[:, g % 2, a:a + 1])
                last.then_inc(exp_done, 1)

            def keep_y(b, g):
                act.wait_ge(mixed, b * GROUPS + (g + 1))
                half, a = g // 2, (g % 2) * GROUP
                nc.scalar.copy(y[0:C, half, a:a + GROUP], mix_bank[0:C, :, 0:C])
                nc.scalar.copy(y[C:128, half, a:a + GROUP], mix_bank[C:128, :, C:128]).then_inc(y_ready, 1)

            def t_high(G, b, par, half):
                act.wait_ge(t_ready, b * 2 + (half + 1))
                if half == 0 and G is not None:
                    act.wait_ge(t_kept, G * 32 + 64)
                nc.scalar.copy(th[:, 1:RP + 1, :, 1 + 64 * half:65 + 64 * half],
                               tf[:, par, 2:RP + 2, :, 64 * half:64 * half + 64]).then_inc(th_ready, 1)

            def keep_r(half, use):
                act.wait_ge(proj_done, use + 1)
                patches = slice(half * HALF, half * HALF + HALF)
                src = proj_bank[:].rearrange("c a r s -> c a (r s)")
                nc.scalar.copy(rbd[0:C, patches, 0], src[0:C])
                nc.scalar.copy(rbd[C:128, patches, 1], src[C:128]).then_inc(r_ready, 1)

            def keep_turned(b, g):
                act.wait_ge(turned, b * GROUPS + (g + 1))
                nc.scalar.copy(probt[:, g % 2], turn_bank[0:KEYS]).then_inc(probt_ready, 1)

            def relu_u(G, k, i):
                act.wait_ge(tile_done, tiles_done(G, i))
                bank = conv_bank[BANK[i]][:].rearrange("c (s w) -> c s w", w=W)
                regions = [(FULL, 0, RP)]
                if k == 0:
                    regions = [(FULL, 1, RP), (slice(C, 128), 0, 1)]
                if k == BANDS:
                    regions = [(slice(0, C), 0, 1)]
                if k in (0, BANDS):
                    outside = slice(0, C) if k == 0 else slice(C, 128)
                    nc.scalar.copy(relued[outside, 0, i, 1:1 + W], zeros[outside, 0, 0])
                for parts, lo, hi in regions:
                    last = nc.scalar.activation(relued[parts, lo:hi, i, 1:1 + W], bank[parts, lo:hi], ACT.Relu,
                                                bias=bias[parts, 0:1])
                last.then_inc(act_read, 1)

            def keep_m2(G, k, which):
                lo, hi = pairs3(k) if which == CONV3 else pairs2(k)
                act.wait_ge(tile_done, tiles_done(G, first_tile(which)))
                bank = conv_bank[BANK[first_tile(which)]][:].rearrange("c (s i w) -> c s i w", i=2, w=WT)
                nc.scalar.copy(m2_sb[:, which % 2, lo:hi], bank[:, lo:hi]).then_inc(act_read, 1)

            def relu_sums(G, k, which):
                lo, hi = pairs3(k) if which == CONV3 else pairs2(k)
                act.wait_ge(dve_read, dve_reads(G, 3 * which + 3))
                src = sums[which][:, lo:hi]
                if which == CONV3:
                    dst = src
                else:
                    act.wait_ge(d_done, G * 3 + which)
                    dst = relued[:, lo:hi, :, 1:1 + W]
                    if k == 0:
                        nc.scalar.copy(relued[:, 0, :, 1:1 + W], zeros[:, 0])
                    if k == BANDS and which == EVEN:
                        nc.scalar.copy(relued[:, 1, :, 1:1 + W], zeros[:, 0])
                nc.scalar.activation(dst, src, ACT.Relu,
                                     bias=bias[:, 2:3] if which == CONV3 else bias[:, 1:2]).then_inc(relu_done, 1)

            def high(G, n):
                act.wait_ge(d_done, G * 3 + (n + 1))
                if n == 0:
                    act.wait_ge(u_kept, G * 32 + 32)
                if n == 1:
                    act.wait_ge(v_kept, G * 64 + 64)
                dst, at = (duh, 1) if n == 0 else (dvh[n - 1], 3 - n)
                for s in (0, 2):
                    last = nc.scalar.copy(dst[:, at + s:at + s + 2], d[n][:, s:s + 2])
                last.then_inc(high_done, 1)

            act.wait_ge(const_in, 16 * 9)
            act.wait_ge(zeroed, 1)
            for half in range(2):
                keep_r(half, half)
            exps(0, 0)
            exps(0, 1)
            keep_turned(0, 0)
            exps(0, 2)
            keep_turned(0, 1)
            keep_y(0, 0)
            exps(0, 3)
            keep_turned(0, 2)
            keep_y(0, 1)
            keep_turned(0, 3)
            keep_y(0, 2)
            keep_r(0, 3)
            keep_y(0, 3)
            for half in range(2):
                t_high(None, 0, 0, half)
            keep_r(1, 5)
            act.wait_ge(v_zeroed, 1)

            def step(G, k, b, q, par, att):
                relu_u(G, k, 0)
                if att:
                    exps(b, 0)
                relu_u(G, k, 1)
                if att:
                    exps(b, 1)
                keep_m2(G, k, CONV3)
                if att:
                    keep_turned(b, 0)
                high(G, 0)
                if att:
                    keep_turned(b, 1)
                    exps(b, 2)
                    keep_y(b, 0)
                    keep_turned(b, 2)
                    exps(b, 3)
                    keep_y(b, 1)
                    keep_turned(b, 3)
                relu_sums(G, k, CONV3)
                if att:
                    keep_y(b, 2)
                keep_m2(G, k, ODD)
                if att:
                    t_high(G, b, par, 0)
                    keep_y(b, 3)
                    keep_r(0, b * 4 + 3)
                relu_sums(G, k, ODD)
                keep_m2(G, k, EVEN)
                if att:
                    t_high(G, b, par, 1)
                    keep_r(1, b * 4 + 5)
                relu_sums(G, k, EVEN)
                high(G, 1)
                high(G, 2)

            schedule(act, step)
            keep_m2(ALL_STEPS, 0, CONV3)
            relu_sums(ALL_STEPS, 0, CONV3)

        @block.vector
        def _(dve):
            def max_scores(b, g):
                dve.wait_ge(scores_done, b * GROUPS + (g + 1))
                nc.vector.tensor_reduce(negmax[:, g % 2],
                                        score_bank[g % 2][:, 0:GROUP * KEYS].rearrange("q (a n) -> q a n", n=KEYS),
                                        AX_X, ALU.max, negate=True).then_inc(max_done, 1)

            def norm(b, g):
                dve.wait_ge(exp_done, b * GROUPS + (g + 1))
                nc.vector.reciprocal(expinv[:, g % 2], expsum[:, g % 2]).then_inc(inv_done, 1)
                dve.wait_ge(inv_done, b * GROUPS + (g + 1))
                inv = expinv[:, g % 2].rearrange("q (a o) -> q a o", o=1).broadcast_to([128, GROUP, KEYS])
                nc.vector.tensor_tensor(prob[:, g % 2], prob[:, g % 2], inv, ALU.mult).then_inc(prob_ready, 1)

            def add_x(G, k, b, par, half, use):
                dve.wait_ge(proj_done, use + 1)
                if half == 0 and G is not None:
                    dve.wait_ge(out_ready, G + 1)
                if half == 0 and k:
                    dve.wait_ge(carried, b * 16 + (16 if k == BANDS else 0))
                for i in range(2):
                    src = slice(i * C, i * C + C)
                    for odd in range(2):
                        o = tf[odd * C:odd * C + C, par, 2:RP + 2, i, 64 * half:64 * half + 64]
                        a = proj_bank[src, :, odd::2, :].rearrange("c a r s -> c r a s")
                        x = xc[src, par, 1 + odd:1 + BAND:2, 1 + 64 * half:65 + 64 * half]
                        last = nc.vector.tensor_tensor(o.rearrange("c r (a s) -> c r a s", s=PATCH), a,
                                                       x.rearrange("c r (a s) -> c r a s", s=PATCH), ALU.add)
                last.then_inc(t_ready, 1)

            def t_low(b, par, half):
                dve.wait_ge(th_ready, b * 2 + (half + 1))
                cols = slice(1 + 64 * half, 65 + 64 * half)
                nc.vector.tensor_tensor(tl[:, 1:RP + 1, :, cols], tf[:, par, 2:RP + 2, :, 64 * half:64 * half + 64],
                                        th[:, 1:RP + 1, :, cols].bitcast(F32), ALU.subtract).then_inc(tl_ready, 1)

            def streams(which, k, n):
                lo, hi = pairs3(k) if which == CONV3 else pairs2(k)
                bank = conv_bank[BANK[first_tile(which) + n]][:].rearrange("c (s i w) -> c s i w", i=2, w=WT)
                left, right = sums[which][:, lo:hi, :, 0::2], sums[which][:, lo:hi, :, 1::2]
                return bank[:, lo:hi], left, right, m2_sb[:, which % 2, lo:hi]

            def middle(G, k, which):
                m1, left, right, m2 = streams(which, k, 1)
                dve.wait_ge(act_read, act_reads(G, 3 + which))
                dve.wait_ge(tile_done, tiles_done(G, first_tile(which) + 1))
                if which == CONV3:
                    dve.wait_ge(sent, G * 16 + 16)
                if which == EVEN:
                    dve.wait_ge(relu_done, G * 3 + 2)
                nc.vector.tensor_tensor(left, m1, m2, ALU.add).then_inc(sum_done, 1)
                nc.vector.tensor_tensor(right, m1, m2, ALU.subtract).then_inc(dve_read, 1)

            def add_m0(G, k, which):
                m0, left, _, _ = streams(which, k, 2)
                dve.wait_ge(tile_done, tiles_done(G, first_tile(which) + 2))
                dve.wait_ge(sum_done, G * 3 + (which + 1))
                nc.vector.tensor_tensor(left, m0, left, ALU.add).then_inc(dve_read, 1)

            def less_m3(G, k, which):
                m3, _, right, _ = streams(which, k, 3)
                dve.wait_ge(tile_done, tiles_done(G, first_tile(which) + 3))
                dve.wait_ge(dve_read, dve_reads(G, 3 * which + 1))
                nc.vector.tensor_tensor(right, right, m3, ALU.subtract).then_inc(dve_read, 1)

            def inputs(G, n, parts=(0, 1)):
                to = d[n % 3]
                col = [relued[:, :, :, c:c + W - 1:2] for c in range(4)]
                if 0 in parts:
                    dve.wait_ge(low_done, G * 3 + (n + 2 if n % 3 else 3))
                    if n == 0:
                        dve.wait_ge(act_read, act_reads(G, 2))
                    else:
                        dve.wait_ge(relu_done, G * 3 + (n + 1))
                    nc.vector.tensor_tensor(to[:, :, 2], col[2], col[1], ALU.subtract)
                    nc.vector.tensor_tensor(to[:, :, 1], col[1], col[2], ALU.add)
                if 1 in parts:
                    nc.vector.tensor_tensor(to[:, :, 0], col[0], col[2], ALU.subtract)
                    nc.vector.tensor_tensor(to[:, :, 3], col[1], col[3], ALU.subtract).then_inc(d_done, 1)

            def low(G, n):
                dve.wait_ge(high_done, G * 3 + (n + 4))
                which = n % 3
                high_part, low_part, at = (dvh[which - 1], dvl[which - 1], 3 - which) if which else (duh, dul, 1)
                for s in (0, 2):
                    last = nc.vector.tensor_tensor(low_part[:, at + s:at + s + 2], d[which][:, s:s + 2],
                                                   high_part[:, at + s:at + s + 2].bitcast(F32), ALU.subtract)
                last.then_inc(low_done, 1)

            def finish(G, k, b):
                lo, hi = pairs3(k)
                dve.wait_ge(relu_done, G * 3 + 1)
                dve.wait_ge(carried, b * 16 if k in (0, BANDS) else b * 16 - 16)
                o = sums[CONV3][:, lo:hi]
                nc.vector.tensor_tensor(o, o, tf[:, 1 - k % 2 if k else 0, lo:hi], ALU.add).then_inc(out_ready, 1)

            nc.vector.memset(rbd[:], 0.0)
            for t in (th, tl):
                nc.vector.memset(t[:, :, :, 0:1].bitcast(F32), 0.0)
                nc.vector.memset(t[:, :, :, WP - 1:WP].bitcast(F32), 0.0)
            for c in (0, WP - 1):
                nc.vector.memset(relued[:, :, :, c:c + 1], 0.0)
            nc.vector.memset(tf[:, 0, 0:2], 0.0)
            nc.vector.memset(qk[:], 0.0).then_inc(zeroed, 1)
            dve.wait_ge(zeroed, 1)
            dve.wait_ge(qk_done, 1)
            nc.vector.tensor_copy(qk[0:C, 0:C], score_bank[0][0:C, 0:C])
            nc.vector.tensor_copy(qk[C:128, C:128], score_bank[0][C:128, 0:C]).then_inc(qk_ready, 1)

            def split_weights():
                dve.wait_ge(w_in, 48)
                nc.vector.tensor_copy(w1h[:], w1_raw).then_inc(w_stage, 1)
                dve.wait_ge(w_stage, 1)
                nc.vector.tensor_tensor(w1l[:], w1_raw, w1h[:].bitcast(F32), ALU.subtract)
                for n, (raw, wh, wl) in enumerate(((w2_raw, w2h, w2l), (w3_raw, w3h, w3l))):
                    g0, g1, g2 = (raw[:, :, t] for t in range(3))
                    nc.vector.tensor_tensor(w_half[:], g0, g2, ALU.add).then_inc(w_stage, 1)
                    dve.wait_ge(w_stage, 3 * n + 2)
                    for m, sign in ((0, 1.0), (1, -1.0)):
                        last = nc.vector.scalar_tensor_tensor(w_mid[:, m], g1, sign, w_half[:], ALU.mult, ALU.add)
                    last.then_inc(w_stage, 1)
                    dve.wait_ge(w_stage, 3 * n + 3)
                    parts = ((0, g0, 1.0), (1, w_mid[:, 0], 0.5), (2, w_mid[:, 1], 0.5), (3, g2, 1.0))
                    for m, g, scale in parts:
                        last = nc.vector.tensor_scalar(wh[:, m], g, scale, None, ALU.mult)
                    last.then_inc(w_stage, 1)
                    dve.wait_ge(w_stage, 3 * n + 4)
                    for m, g, scale in parts:
                        last = nc.vector.scalar_tensor_tensor(wl[:, m], g, scale, wh[:, m].bitcast(F32),
                                                              ALU.mult, ALU.subtract)
                return last

            max_scores(0, 0)
            max_scores(0, 1)
            norm(0, 0)
            norm(0, 1)
            max_scores(0, 2)
            norm(0, 2)
            max_scores(0, 3)
            norm(0, 3)
            add_x(None, 0, 0, 0, 0, 2)
            add_x(None, 0, 0, 0, 1, 4)
            for half in range(2):
                t_low(0, 0, half)
            split_weights().then_inc(split_done, 1)

            def step(G, k, b, q, par, att):
                if k:
                    inputs(G, 2 - 3)
                    low(G, 1 - 3)
                if att:
                    max_scores(b, 0)
                if k:
                    low(G, 2 - 3)
                if att:
                    norm(b, 0)
                    max_scores(b, 1)
                inputs(G, 0)
                if att:
                    norm(b, 1)
                middle(G, k, CONV3)
                if att:
                    max_scores(b, 2)
                low(G, 0)
                if att:
                    norm(b, 2)
                add_m0(G, k, CONV3)
                if att:
                    max_scores(b, 3)
                    norm(b, 3)
                less_m3(G, k, CONV3)
                finish(G, k, b)
                if att:
                    add_x(G, k, b, par, 0, b * 4 + 2)
                middle(G, k, ODD)
                if att:
                    t_low(b, par, 0)
                add_m0(G, k, ODD)
                less_m3(G, k, ODD)
                if att:
                    add_x(G, k, b, par, 1, b * 4 + 4)
                inputs(G, 1, (0,))
                middle(G, k, EVEN)
                if att:
                    t_low(b, par, 1)
                add_m0(G, k, EVEN)
                inputs(G, 1, (1,))
                less_m3(G, k, EVEN)
                if k == BANDS:
                    inputs(G, 2)
                    low(G, 1)
                    low(G, 2)

            schedule(dve, step)
            middle(ALL_STEPS, 0, CONV3)
            add_m0(ALL_STEPS, 0, CONV3)
            less_m3(ALL_STEPS, 0, CONV3)
            finish(ALL_STEPS, 0, PAIRS * BANDS + 1)

        @block.gpsimd
        def _(pool):
            nc.gpsimd.memset(zeros[:], 0.0)
            for t in (*dvh, *dvl):
                nc.gpsimd.memset(t[:].bitcast(F32), 0.0)
            for i, (credit, n) in enumerate(((act_read, ACT_READS), (dve_read, DVE_READS), (high_done, 3), (low_done, 3), (sent, 16),
                                             (t_kept, 32), (u_kept, 32), (carried, 16), (v_zeroed, 1))):
                nc.gpsimd.memset(credits[:, i:i + 1], 0.0).then_inc(credit, n)


def kernel(**inputs):
    import concourse.bacc as bacc
    from concourse.bass_utils import run_bass_kernel_spmd

    given = {n.removeprefix("L0_conv_"): np.asarray(a) for n, a in inputs.items()}
    f32 = np.float32

    padded = np.zeros((PAIRS, 2, H + 2, WP, C), f32)
    padded[:, :, 1:-1, 1:-1] = given["x"].reshape(2, PAIRS, H, W, C).swapaxes(0, 1)
    x_bands = np.zeros((LOADS, 128, HALO, WP), f32)
    x_keys = np.zeros((LOADS, HALO, HALO, PATCHES, 2, C), f32)
    for n in range(PAIRS * BANDS):
        p, row = n // BANDS, n % BANDS * BAND
        band = padded[p, :, row:row + HALO]
        x_bands[n] = band.transpose(0, 3, 1, 2).reshape(128, HALO, WP)
        for a in range(PATCHES):
            x_keys[n, :, :, a] = band[:, :, a * PATCH:a * PATCH + HALO].transpose(1, 2, 0, 3)

    vbd = np.zeros((128, 128), f32)
    vbd[:C, :C] = vbd[C:, C:] = given["V_P"]
    k1, k2, k3 = (given[f"ff{i}_kernel"] for i in (1, 2, 3))
    w1 = np.zeros((128, 2, 3, 128), f32)
    w2 = np.zeros((128, 4, 3, 128), f32)
    w3 = np.zeros((128, 4, 3, 128), f32)
    for c in range(3):
        for s in range(2):
            for i in range(2):
                for o in range(2):
                    tap = 2 * s + i - o
                    if 0 <= tap < 3:
                        w1[i * C:i * C + C, s, c, o * C:o * C + C] = k1[tap, c]
        for even in range(2):
            for s in range(2):
                for i in range(2):
                    tap = 2 * s + i - (0 if even else 1)
                    if 0 <= tap < 3:
                        w2[i * C:i * C + C, 2 * even + s, c] = k2[tap, c]
        for s in range(4):
            for o in range(2):
                if 0 <= s - o < 3:
                    w3[:, s, c, o * C:o * C + C] = k3[s - o, c]

    window = np.full((2, PATCH, PATCH, HALO, HALO), NEG, f32)
    for r in range(PATCH):
        for c in range(PATCH):
            window[:, r, c, r:r + 3, c:c + 3] = 0.0

    bf16 = mybir.dt.np(BF16)
    data = {
        "x_bands": x_bands,
        "x_keys": x_keys.reshape(LOADS, KEYS, PATCHES, 128),
        "qt2": np.concatenate([given["Q_P"].T, given["Q_P"].T], axis=1),
        "kt": given["K_P"].T,
        "vbd": vbd,
        "w1": w1.reshape(128, 6, 128),
        "w2": w2,
        "w3": w3,
        "b1": np.concatenate([given["ff1_bias"]] * 2).reshape(128, 1),
        "b2": given["ff2_bias"].reshape(128, 1),
        "b3": np.concatenate([given["ff3_bias"]] * 2).reshape(128, 1),
        "window": window.reshape(128, KEYS).astype(bf16),
        "eye": np.eye(128, dtype=f32),
        "eye16": np.eye(128, dtype=f32).astype(bf16),
    }
    nc = bacc.Bacc("TRN2", target_bir_lowering=False, num_devices=1)
    arrays, args = {}, []
    for name, a in data.items():
        arrays[name] = np.ascontiguousarray(a)
        args.append(nc.dram_tensor(name, a.shape, mybir.dt.from_np(a.dtype), kind="ExternalInput").ap())
    out = nc.dram_tensor("out", (128, ALL_STEPS + 1, RP, 2, W), F32, kind="ExternalOutput").ap()
    build(nc, *args, out)
    got = run_bass_kernel_spmd(nc, [arrays], core_ids=[0]).results[0]["out"]
    got = got[:, 1:].reshape(2, C, PAIRS, STEPS * RP, 2, W)[:, :, :, 2:2 + H // 2]
    return np.ascontiguousarray(got.transpose(4, 2, 3, 0, 5, 1)).reshape(IMAGES, H, W, C)
```

```python
from contextlib import ExitStack

import concourse.bass as bass
from concourse import mybir
import numpy as np

F32 = mybir.dt.float32
F32R = mybir.dt.float32r
BF16 = mybir.dt.bfloat16
ALU = mybir.AluOpType
ACT = mybir.ActivationFunctionType
AX_X = mybir.AxisListType.X

IMAGES, H, W, C = 8, 128, 128, 64
PAIRS = IMAGES // 2
BAND = 8
BANDS = H // BAND
STEPS = BANDS + 1
ALL_STEPS = PAIRS * STEPS
PATCH = 8
HALO = PATCH + 2
KEYS = HALO * HALO
PATCHES = W // PATCH
GROUP = 4
GROUPS = PATCHES // GROUP
HALF = PATCHES // 2
WP = W + 2
WT = W // 2
RP = BAND // 2
LOADS = PAIRS * BANDS + 3
NEG = -3.0e38
FULL = slice(0, 128)

STREAMS = (2, 1, 0, 3)
PARTS = (slice(1, 3), slice(0, 4, 3))
CONV1, CONV3, ODD, EVEN = range(4)
SETS, TILES = 4, 16
BANK = (0, 1, 2, 0, 1, 2, 0, 2, 1, 0, 2, 1, 0, 2, 1, 2)
FROM1, FROM_ODD, FROM_EVEN, FROM_T = range(4)
ACT_READS, DVE_READS = SETS, 3 * SETS
READ = {}
for _set in range(SETS):
    READ[4 * _set] = ("act", 1 + _set)
    for _n in range(3):
        READ[4 * _set + 1 + _n] = ("dve", 3 * _set + _n + 1)


def first_tile(which):
    return 4 * which


def pairs1(k):
    return (0, 1) if k == BANDS else (0, RP)


def pairs2(k):
    return (1, RP) if k == 0 else (0, 1) if k == BANDS else (0, RP)


def pairs3(k):
    return (2, RP) if k == 1 else (0, 2) if k == 0 else (0, RP)


def new_slots(n, k):
    return {FROM1: 1, FROM_ODD: 1, FROM_EVEN: 2}[n] if k == BANDS else RP


def pairs(which, k):
    return (pairs1, pairs3, pairs2, pairs2)[which](k)


def build(nc, x_bands, x_keys, qt2, kt, vbd, w1, w2, w3, b1, b2, b3, window, eye, eye16, out):
    with ExitStack() as ctx:
        def sb(name, shape, dt):
            return ctx.enter_context(nc.sbuf_tensor(name, shape, dt))

        def pb(name, shape):
            return ctx.enter_context(nc.psum_tensor(name, shape, F32))

        def sem(name):
            return ctx.enter_context(nc.semaphore(name))

        qt_sb = sb("qt_sb", [C, 128], F32)
        kt_sb = sb("kt_sb", [C, C], F32)
        qk = sb("qk", [128, 128], F32)
        v_sb = sb("v_sb", [128, 128], F32)
        w1h = sb("w1h", [128, 4, 2, 128], F32R)
        w1l = sb("w1l", [128, 4, 2, 128], F32R)
        w2h = sb("w2h", [128, 4, 4, 128], F32R)
        w2l = sb("w2l", [128, 4, 4, 128], F32R)
        w3h = sb("w3h", [128, 4, 4, 128], F32R)
        w3l = sb("w3l", [128, 4, 4, 128], F32R)
        bias = sb("bias", [128, 3], F32)
        window_sb = sb("window_sb", [128, KEYS], BF16)
        eye_sb = sb("eye_sb", [128, 128], F32)
        eye16_sb = sb("eye16_sb", [128, 128], BF16)
        zeros = sb("zeros", [128, 1, 2, W], F32)
        credits = sb("credits", [128, 16], F32)
        xc = sb("xc", [128, 2, HALO, WP], F32)
        xk = sb("xk", [KEYS, PATCHES, 128], F32)
        rbd = sb("rbd", [128, PATCHES, 2, C], F32)
        negmax = sb("negmax", [128, 2, GROUP], F32)
        expsum = sb("expsum", [128, 2, GROUP], F32)
        expinv = sb("expinv", [128, 2, GROUP], F32)
        prob = sb("prob", [128, 2, GROUP, KEYS], F32)
        probt = sb("probt", [KEYS, 2, GROUP, 128], F32)
        y = sb("y", [128, HALF, C], F32)
        tf = sb("tf", [128, 2, RP + 2, 2, WP], F32)
        relued = sb("relued", [128, RP, 2, WP], F32)
        m2_sb = sb("m2_sb", [128, RP, 2, WT], F32)
        work = sb("work", [128, 6 * RP * 2 * W], F32)
        size = RP * 2 * W
        d = [work[:, n * 2 * size:(n + 1) * 2 * size].rearrange("c (s m i w) -> c s m i w", s=RP, m=4, i=2)
             for n in (0, 1, 0, 0)]
        sums = [work[:, n * size:(n + 1) * size].rearrange("c (s i w) -> c s i w", s=RP, i=2)
                for n in (4, 4, 5, 5)]
        dth = sb("dth", [128, RP + 1, 4, 2, WT], F32R)
        dtl = sb("dtl", [128, RP + 1, 4, 2, WT], F32R)
        duh = sb("duh", [128, RP + 1, 4, 2, WT], F32R)
        dul = sb("dul", [128, RP + 1, 4, 2, WT], F32R)
        dvh = [sb(f"dvh{i}", [128, RP + 2 - i, 4, 2, WT], F32R) for i in range(2)]
        dvl = [sb(f"dvl{i}", [128, RP + 2 - i, 4, 2, WT], F32R) for i in range(2)]
        d_high, d_low, new_slot = (duh, *dvh, dth), (dul, *dvl, dtl), (1, 2, 1, 1)
        at = 0
        raws = []
        for slots in (2, 4, 4):
            n = slots * 3 * 128
            raws.append(work[:, at:at + n].rearrange("c (s t n) -> c s t n", s=slots, t=3))
            at += n
        w_mid = work[:, at:at + 1024].rearrange("c (m s n) -> c m s n", m=2, s=4)
        w_half = work[:, at + 1024:at + 1536].rearrange("c (s n) -> c s n", s=4)
        w3_mid = relued[:, :, :, 1:1 + W].rearrange("c s m n -> c m s n")
        w3_half = work[:, at + 1536:at + 2048].rearrange("c (s n) -> c s n", s=4)

        conv_bank = [pb(f"conv_bank{i}", [128, 512]) for i in range(3)]
        score_bank = [pb(f"score_bank{i}", [128, 512]) for i in range(2)]
        turn_bank = pb("turn_bank", [128, GROUP, 128])
        mix_bank = pb("mix_bank", [128, GROUP, 128])
        proj_bank = pb("proj_bank", [128, HALF, PATCH, PATCH])

        const_in = sem("const_in")
        w_in = sem("w_in")
        w_stage = sem("w_stage")
        w3_stage = sem("w3_stage")
        split_done = sem("split_done")
        zeroed = sem("zeroed")
        v_zeroed = sem("v_zeroed")
        qk_done = sem("qk_done")
        qk_ready = sem("qk_ready")
        xc_in = [sem(f"xc{i}_in") for i in range(2)]
        xk_in = sem("xk_in")
        proj_done = sem("proj_done")
        r_ready = sem("r_ready")
        scores_done = sem("scores_done")
        max_done = sem("max_done")
        exp_done = sem("exp_done")
        inv_done = sem("inv_done")
        prob_ready = sem("prob_ready")
        turned = sem("turned")
        probt_ready = sem("probt_ready")
        mixed = sem("mixed")
        y_ready = sem("y_ready")
        t_ready = sem("t_ready")
        tile_done = sem("tile_done")
        act_read = sem("act_read")
        dve_read = sem("dve_read")
        sum_done = sem("sum_done")
        relu_done = sem("relu_done")
        names = ("from1", "from_odd", "from_even", "from_t")
        d_done = [sem(f"{n}_d_done") for n in names]
        high_done = [sem(f"{n}_high_done") for n in names]
        low_done = [sem(f"{n}_low_done") for n in names]
        out_ready = sem("out_ready")
        sent = sem("sent")
        t_kept = sem("t_kept")
        u_kept = sem("u_kept")
        v_kept = sem("v_kept")
        carried = sem("carried")

        block = ctx.enter_context(nc.Block())

        def schedule(eng, step):
            with eng.Fori(0, PAIRS) as p:
                g0, b0, q0 = p * STEPS, p * BANDS, p * (BANDS // 2)
                step(g0, 0, b0 + 1, q0, 1, True)
                step(g0 + 1, 1, b0 + 2, q0 + 1, 0, True)
                with eng.Fori(0, (BANDS - 4) // 2) as h:
                    for j in range(2):
                        step(g0 + h * 2 + (2 + j), 2 + j, b0 + h * 2 + (3 + j), q0 + h + (1 + j), 1 - j, True)
                step(g0 + (BANDS - 2), BANDS - 2, b0 + (BANDS - 1), q0 + (BANDS // 2 - 1), 1, True)
                step(g0 + (BANDS - 1), BANDS - 1, b0 + BANDS, q0 + BANDS // 2, 0, False)
                step(g0 + BANDS, BANDS, b0 + BANDS, q0 + BANDS // 2, 0, True)

        def tiles_done(G, tile):
            return G * TILES + (tile + 1 - (4 if G is ALL_STEPS else 0))

        def act_reads(G, n):
            return G * ACT_READS + (ACT_READS + n - (1 if G is ALL_STEPS else 0))

        def dve_reads(G, n):
            return G * DVE_READS + (DVE_READS + n - (3 if G is ALL_STEPS else 0))

        def sets_done(G, which):
            return G * SETS + (which + 1 - (1 if G is ALL_STEPS else 0))

        def parts_done(G, n, part, behind=0):
            return G * 2 + (part + 1 - 2 * behind)

        def splits_done(G, n, part, behind=0):
            return G * 2 + (part + 1 - 2 * behind + (2 if n in (FROM_ODD, FROM_EVEN) else 0))

        def split_weights(engine, wait, raw, wh, wl, mid, half, stage, before):
            g0, g1, g2 = (raw[:, :, t] for t in range(3))
            engine.tensor_tensor(half, g0, g2, ALU.add).then_inc(stage, 1)
            wait(stage, before + 1)
            engine.tensor_tensor(mid[:, 0], half, g1, ALU.add)
            engine.tensor_tensor(mid[:, 1], half, g1, ALU.subtract).then_inc(stage, 1)
            wait(stage, before + 2)
            engine.tensor_scalar(mid, mid, 0.5, None, ALU.mult).then_inc(stage, 1)
            wait(stage, before + 3)
            parts = ((0, g0), (1, mid[:, 0]), (2, mid[:, 1]), (3, g2))
            for m, g in parts:
                last = engine.tensor_copy(wh[:, m], g)
            last.then_inc(stage, 1)
            wait(stage, before + 4)
            for m, g in parts:
                last = engine.tensor_tensor(wl[:, m], g, wh[:, m].bitcast(F32), ALU.subtract)
            return last

        @block.sync
        def _(sp):
            for dst, src in ((qt_sb, qt2), (kt_sb, kt), (v_sb, vbd), (window_sb, window), (eye_sb, eye),
                             (eye16_sb, eye16)):
                sp.dma_start(dst[:], src).then_inc(const_in, 16)
            for i, src in enumerate((b1, b2, b3)):
                sp.dma_start(bias[:, i:i + 1], src).then_inc(const_in, 16)

            def move(t, to, at, n):
                return sp.dma_start(t[:, to:to + n].bitcast(F32), t[:, at:at + n].bitcast(F32))

            def load_xc(b, par):
                sp.dma_start(xc[:, par], x_bands[b]).then_inc(xc_in[par], 16)

            def load_xk(b):
                sp.dma_start(xk[:], x_keys[b]).then_inc(xk_in, 16)

            load_xc(0, 0)
            load_xk(0)
            load_xc(1, 1)
            for dst, src in zip(raws, (w1, w2, w3)):
                sp.dma_start(dst, src).then_inc(w_in, 16)
            sp.wait_ge(mixed, GROUPS)
            load_xk(1)
            sp.wait_ge(t_ready, 2)
            load_xc(2, 0)

            def store(G, k):
                lo, hi = pairs3(k)
                sp.wait_ge(out_ready, G + 1)
                sp.dma_start(out[:, G, lo:hi], sums[CONV3][:, lo:hi]).then_inc(sent, 16)

            def step(G, k, b, q, par, att):
                if k:
                    if k < BANDS:
                        sp.wait_ge(t_ready, b * 2)
                    else:
                        sp.wait_ge(out_ready, G)
                    sp.dma_start(tf[:, k % 2, 0:2], tf[:, 1 - k % 2, RP:RP + 2]).then_inc(carried, 16)
                sp.wait_ge(tile_done, tiles_done(G, 3))
                for t in (dth, dtl):
                    move(t, 0, RP, 1).then_inc(t_kept, 16)
                sp.wait_ge(tile_done, tiles_done(G, 7))
                for t in (dvh, dvl):
                    move(t[0], 0, RP, 2).then_inc(v_kept, 16)
                    move(t[1], 0, RP, 1).then_inc(v_kept, 16)
                store(G, k)
                if att:
                    sp.wait_ge(mixed, b * GROUPS + GROUPS)
                    load_xk(b + 1)
                    sp.wait_ge(t_ready, b * 2 + 2)
                    load_xc(b + 2, par)
                sp.wait_ge(tile_done, tiles_done(G, 15))
                for t in (duh, dul):
                    move(t, 0, RP, 1).then_inc(u_kept, 16)

            schedule(sp, step)
            store(ALL_STEPS, 0)
            sp.wait_ge(sent, 16 * (ALL_STEPS + 2))
            sp.wait_ge(t_kept, 32 * (ALL_STEPS + 1))
            sp.wait_ge(u_kept, 32 * (ALL_STEPS + 1))
            sp.wait_ge(v_kept, 64 * ALL_STEPS)
            sp.wait_ge(carried, 16 * (PAIRS * BANDS + 1))
            sp.wait_ge(xk_in, 16 * (LOADS - 1))
            for i in range(2):
                sp.wait_ge(xc_in[i], 16 * ((LOADS + 1 - i) // 2))

        @block.tensor
        def _(pe):
            def proj(weights, moving):
                nc.tensor.matmul(proj_bank[:], weights, moving, start=True, stop=True).then_inc(proj_done, 1)

            def r_product(b, par, half):
                if half:
                    pe.wait_ge(r_ready, b * 2 + 1)
                elif not isinstance(b, int) or b:
                    pe.wait_ge(t_ready, b * 2)
                band = xc[:, par, 1:1 + BAND, 1 + half * 64:65 + half * 64]
                proj(qk[:], band.rearrange("c r (a s) -> c a r s", s=PATCH))

            def v_product(b, half):
                pe.wait_ge(y_ready, b * GROUPS + 2 * (half + 1))
                if half:
                    pe.wait_ge(t_ready, b * 2 + 1)
                else:
                    pe.wait_ge(r_ready, b * 2 + 2)
                proj(v_sb[:], y[:])

            def scores(b, par, g):
                pe.wait_ge(r_ready, b * 2 + (g // 2 + 1))
                if not (isinstance(b, int) and g < 2):
                    pe.wait_ge(exp_done, b * GROUPS + (g - 1))
                bank = score_bank[g % 2][:, 0:GROUP * KEYS].rearrange("q (a n) -> q a n", n=KEYS)
                nc.tensor.matmul(bank, eye16_sb[:],
                                 window_sb[:].rearrange("q (o n) -> q o n", o=1).broadcast_to([128, GROUP, KEYS]),
                                 start=True, stop=False)
                for a in range(GROUP):
                    patch = g * GROUP + a
                    last = nc.tensor.matmul(bank[:, a], rbd[:, patch],
                                            xc[:, par, :, patch * PATCH:patch * PATCH + HALO],
                                            start=False, stop=a == GROUP - 1)
                last.then_inc(scores_done, 1)

            def turn(b, g):
                pe.wait_ge(prob_ready, b * GROUPS + (g + 1))
                if not (isinstance(b, int) and g == 0):
                    pe.wait_ge(probt_ready, b * GROUPS + g)
                for a in range(GROUP):
                    last = nc.tensor.transpose(turn_bank[0:KEYS, a], prob[:, g % 2, a], eye_sb[:])
                last.then_inc(turned, 1)

            def mix(b, g):
                if g == 0:
                    pe.wait_ge(xk_in, b * 16 + 16)
                pe.wait_ge(probt_ready, b * GROUPS + (g + 1))
                if not (isinstance(b, int) and g == 0):
                    pe.wait_ge(y_ready, b * GROUPS + g)
                for a in range(GROUP):
                    last = nc.tensor.matmul(mix_bank[:, a], xk[:, g * GROUP + a], probt[:, g % 2, a],
                                            start=True, stop=True)
                last.then_inc(mixed, 1)

            def tile(G, n, stages):
                who, count = READ[n]
                before = [t for t in range(first_tile(CONV3) if G is ALL_STEPS else 0, n) if BANK[t] == BANK[n]]
                if before:
                    who, count = READ[before[-1]]
                    pe.wait_ge(*(act_read, act_reads(G, count)) if who == "act" else (dve_read, dve_reads(G, count)))
                else:
                    who, count = READ[[t for t in range(TILES) if BANK[t] == BANK[n]][-1]]
                    if who == "act":
                        pe.wait_ge(act_read, G * ACT_READS + count)
                    else:
                        pe.wait_ge(dve_read, G * DVE_READS + count)
                left = sum(len(products) for _, products in stages)
                start = True
                for ready, products in stages:
                    if ready:
                        pe.wait_ge(*ready)
                    for weights, moving, lo, hi in products:
                        left -= 1
                        last = nc.tensor.matmul(conv_bank[BANK[n]][:, lo * 128:hi * 128], weights, moving,
                                                start=start, stop=not left)
                        start = False
                last.then_inc(tile_done, 1)

            def passes(taps, wh, wl, source, m, value, wait):
                def part(t, s, lo, hi):
                    return t[:, lo + s:hi + s, m], lo, hi
                high = [(w[:, m, n], *part(d_high[source], s, lo, hi)) for w in (wh, wl) for n, s, lo, hi in taps]
                low = [(wh[:, m, n], *part(d_low[source], s, lo, hi)) for n, s, lo, hi in taps]
                return [((high_done[source], value) if wait else None, high),
                        ((low_done[source], value) if wait else None, low)]

            def conv1(k, m, value, wait):
                taps = [(1, 1, 0, RP), (0, 0, 1 if k == 0 else 0, RP)] if k < BANDS else [(0, 0, 0, 1)]
                return passes(taps, w1h, w1l, FROM_T, m, value, wait)

            def conv2(k, even, m, value, wait):
                return passes([(2 * even + s, s, *pairs2(k)) for s in range(2)], w2h, w2l, FROM1, m, value, wait)

            def conv3(k, m, value, wait):
                odd, even = (passes([(s, s // 2, *pairs3(k)) for s in (i, i + 2)], w3h, w3l, source, m, value, wait)
                             for i, source in enumerate((FROM_ODD, FROM_EVEN)))
                return [odd[0], even[0], odd[1], even[1]]

            pe.wait_ge(const_in, 16 * 9)
            nc.tensor.matmul(score_bank[0][:, 0:C], qt_sb[:], kt_sb[:], start=True, stop=True).then_inc(qk_done, 1)
            pe.wait_ge(qk_ready, 1)
            pe.wait_ge(xc_in[0], 16)
            for half in range(2):
                r_product(0, 0, half)
            scores(0, 0, 0)
            scores(0, 0, 1)
            turn(0, 0)
            scores(0, 0, 2)
            turn(0, 1)
            mix(0, 0)
            scores(0, 0, 3)
            turn(0, 2)
            mix(0, 1)
            v_product(0, 0)
            turn(0, 3)
            mix(0, 2)
            pe.wait_ge(xc_in[1], 16)
            mix(0, 3)
            v_product(0, 1)
            r_product(1, 1, 0)
            r_product(1, 1, 1)
            pe.wait_ge(split_done, 2)
            pe.wait_ge(v_zeroed, 1)

            def step(G, k, b, q, par, att):
                def set_tile(which, n):
                    m, part = STREAMS[n], n // 2
                    wait = n % 2 == 0 and which != EVEN
                    if which == CONV1:
                        stages = conv1(k, m, b * 2 - (1 - part), wait)
                    elif which == CONV3:
                        stages = conv3(k, m, splits_done(G, FROM_ODD, part, 1), wait)
                    else:
                        stages = conv2(k, which == EVEN, m, splits_done(G, FROM1, part), wait)
                    tile(G, first_tile(which) + n, stages)

                pe.wait_ge(t_kept, G * 32 + 32)
                set_tile(CONV1, 0)
                if att:
                    scores(b, par, 0)
                set_tile(CONV1, 1)
                if att:
                    scores(b, par, 1)
                set_tile(CONV1, 2)
                set_tile(CONV1, 3)
                if att:
                    turn(b, 0)
                    scores(b, par, 2)
                    turn(b, 1)
                    mix(b, 0)
                    scores(b, par, 3)
                set_tile(CONV3, 0)
                set_tile(CONV3, 1)
                if att:
                    turn(b, 2)
                    mix(b, 1)
                set_tile(CONV3, 2)
                if att:
                    turn(b, 3)
                    mix(b, 2)
                    v_product(b, 0)
                set_tile(CONV3, 3)
                if att:
                    mix(b, 3)
                set_tile(ODD, 0)
                set_tile(ODD, 1)
                set_tile(ODD, 2)
                set_tile(ODD, 3)
                if att:
                    v_product(b, 1)
                set_tile(EVEN, 0)
                set_tile(EVEN, 1)
                set_tile(EVEN, 2)
                if att:
                    pe.wait_ge(xc_in[1 - par], (q + (1 + par)) * 16)
                    r_product(b + 1, 1 - par, 0)
                set_tile(EVEN, 3)
                if att:
                    r_product(b + 1, 1 - par, 1)

            schedule(pe, step)
            for n in range(4):
                value = splits_done(ALL_STEPS, FROM_ODD, n // 2, 1)
                tile(ALL_STEPS, first_tile(CONV3) + n, conv3(0, STREAMS[n], value, n % 2 == 0))

        @block.scalar
        def _(act):
            def exps(b, g):
                act.wait_ge(max_done, b * GROUPS + (g + 1))
                for a in range(GROUP):
                    last = nc.scalar.activation(prob[:, g % 2, a], score_bank[g % 2][:, a * KEYS:(a + 1) * KEYS],
                                                ACT.Exp, bias=negmax[:, g % 2, a:a + 1],
                                                accum_out=expsum[:, g % 2, a:a + 1])
                last.then_inc(exp_done, 1)

            def keep_y(b, g):
                act.wait_ge(mixed, b * GROUPS + (g + 1))
                if g == 2:
                    act.wait_ge(proj_done, b * 4 + 3)
                a = (g % 2) * GROUP
                nc.scalar.copy(y[0:C, a:a + GROUP], mix_bank[0:C, :, 0:C])
                nc.scalar.copy(y[C:128, a:a + GROUP], mix_bank[C:128, :, C:128]).then_inc(y_ready, 1)

            def keep_r(half, use):
                act.wait_ge(proj_done, use + 1)
                patches = slice(half * HALF, half * HALF + HALF)
                src = proj_bank[:].rearrange("c a r s -> c a (r s)")
                nc.scalar.copy(rbd[0:C, patches, 0], src[0:C])
                nc.scalar.copy(rbd[C:128, patches, 1], src[C:128]).then_inc(r_ready, 1)

            def keep_turned(b, g):
                act.wait_ge(turned, b * GROUPS + (g + 1))
                nc.scalar.copy(probt[:, g % 2], turn_bank[0:KEYS]).then_inc(probt_ready, 1)

            def keep_m2(G, k, which):
                lo, hi = pairs(which, k)
                act.wait_ge(tile_done, tiles_done(G, first_tile(which)))
                act.wait_ge(dve_read, dve_reads(G, 3 * which - 2))
                bank = conv_bank[BANK[first_tile(which)]][:].rearrange("c (s i w) -> c s i w", i=2, w=WT)
                nc.scalar.copy(m2_sb[:, lo:hi], bank[:, lo:hi]).then_inc(act_read, 1)

            def relu_conv1(G, k):
                act.wait_ge(dve_read, dve_reads(G, 3))
                lo, hi = pairs1(k)
                regions = [(FULL, lo, hi)]
                if k == 0:
                    regions = [(FULL, 1, RP), (slice(C, 128), 0, 1)]
                if k == BANDS:
                    regions = [(slice(0, C), 0, 1)]
                if k in (0, BANDS):
                    outside = slice(0, C) if k == 0 else slice(C, 128)
                    nc.scalar.copy(relued[outside, 0, :, 1:1 + W], zeros[outside, 0])
                for parts, lo, hi in regions:
                    last = nc.scalar.activation(relued[parts, lo:hi, :, 1:1 + W], sums[CONV1][parts, lo:hi], ACT.Relu,
                                                bias=bias[parts, 0:1])
                last.then_inc(relu_done, 1)

            def relu_sums(G, k, which, behind=0):
                lo, hi = pairs(which, k)
                act.wait_ge(dve_read, dve_reads(G, 3 * which + 3 - behind * DVE_READS))
                src = sums[which][:, lo:hi]
                if which == CONV3:
                    dst = src
                else:
                    n = FROM1 if which == ODD else FROM_ODD
                    act.wait_ge(d_done[n], parts_done(G, n, 1, behind))
                    dst = relued[:, lo:hi, :, 1:1 + W]
                    if k == 0:
                        nc.scalar.copy(relued[:, 0, :, 1:1 + W], zeros[:, 0])
                    if k == BANDS and which == EVEN:
                        nc.scalar.copy(relued[:, 1, :, 1:1 + W], zeros[:, 0])
                nc.scalar.activation(dst, src, ACT.Relu,
                                     bias=bias[:, 2:3] if which == CONV3 else bias[:, 1:2]).then_inc(relu_done, 1)

            def high(G, k, n, part, behind=0):
                act.wait_ge(d_done[n], parts_done(G, n, part, behind))
                if n == FROM1 and part == 0:
                    act.wait_ge(u_kept, G * 32 + 32)
                if n == FROM_ODD and part == 0:
                    act.wait_ge(v_kept, G * 64 + (64 - 64 * behind))
                streams, at = PARTS[part], new_slot[n]
                slots = new_slots(n, k)
                nc.scalar.copy(d_high[n][:, at:at + slots, streams], d[n][:, 0:slots, streams]).then_inc(high_done[n], 1)

            def t_high(G, b, part):
                act.wait_ge(d_done[FROM_T], b * 2 + (part + 1))
                if part == 0 and G is not None:
                    act.wait_ge(t_kept, G * 32 + 64)
                streams = PARTS[part]
                nc.scalar.copy(dth[:, 1:RP + 1, streams], d[FROM_T][:, :, streams]).then_inc(high_done[FROM_T], 1)

            act.wait_ge(const_in, 16 * 9)
            act.wait_ge(zeroed, 1)
            for half in range(2):
                keep_r(half, half)
            exps(0, 0)
            exps(0, 1)
            keep_turned(0, 0)
            exps(0, 2)
            keep_turned(0, 1)
            keep_y(0, 0)
            exps(0, 3)
            keep_turned(0, 2)
            keep_y(0, 1)
            keep_turned(0, 3)
            keep_y(0, 2)
            keep_y(0, 3)
            for n in range(2):
                t_high(None, 0, n)
                keep_r(n, 4 + n)
            act.wait_ge(v_zeroed, 1)

            def step(G, k, b, q, par, att):
                keep_m2(G, k, CONV1)
                if att:
                    exps(b, 0)
                    exps(b, 1)
                if k:
                    relu_sums(G, k - 1, EVEN, 1)
                if att:
                    keep_turned(b, 0)
                if k:
                    high(G, k - 1, FROM_ODD, 0, 1)
                    high(G, k - 1, FROM_EVEN, 0, 1)
                if att:
                    keep_turned(b, 1)
                    exps(b, 2)
                    keep_y(b, 0)
                if k:
                    high(G, k - 1, FROM_ODD, 1, 1)
                if att:
                    exps(b, 3)
                if k:
                    high(G, k - 1, FROM_EVEN, 1, 1)
                keep_m2(G, k, CONV3)
                relu_conv1(G, k)
                if att:
                    keep_turned(b, 2)
                    keep_y(b, 1)
                high(G, k, FROM1, 0)
                if att:
                    keep_turned(b, 3)
                high(G, k, FROM1, 1)
                if att:
                    keep_y(b, 2)
                relu_sums(G, k, CONV3)
                if att:
                    keep_y(b, 3)
                keep_m2(G, k, ODD)
                keep_m2(G, k, EVEN)
                relu_sums(G, k, ODD)
                if att:
                    t_high(G, b, 0)
                    keep_r(0, b * 4 + 4)
                    t_high(G, b, 1)
                    keep_r(1, b * 4 + 5)
                if k == BANDS:
                    for part in range(2):
                        high(G, k, FROM_ODD, part)
                    relu_sums(G, k, EVEN)
                    for part in range(2):
                        high(G, k, FROM_EVEN, part)

            schedule(act, step)
            keep_m2(ALL_STEPS, 0, CONV3)
            relu_sums(ALL_STEPS, 0, CONV3)

        @block.vector
        def _(dve):
            def max_scores(b, g):
                dve.wait_ge(scores_done, b * GROUPS + (g + 1))
                nc.vector.tensor_reduce(negmax[:, g % 2],
                                        score_bank[g % 2][:, 0:GROUP * KEYS].rearrange("q (a n) -> q a n", n=KEYS),
                                        AX_X, ALU.max, negate=True).then_inc(max_done, 1)

            def norm(b, g):
                dve.wait_ge(exp_done, b * GROUPS + (g + 1))
                nc.vector.reciprocal(expinv[:, g % 2], expsum[:, g % 2]).then_inc(inv_done, 1)
                dve.wait_ge(inv_done, b * GROUPS + (g + 1))
                inv = expinv[:, g % 2].rearrange("q (a o) -> q a o", o=1).broadcast_to([128, GROUP, KEYS])
                nc.vector.tensor_tensor(prob[:, g % 2], prob[:, g % 2], inv, ALU.mult).then_inc(prob_ready, 1)

            def add_x(G, k, b, par, half, use):
                dve.wait_ge(proj_done, use + 1)
                if half == 0 and G is not None:
                    dve.wait_ge(out_ready, G + 1)
                if half == 0 and k:
                    dve.wait_ge(carried, b * 16 + (16 if k == BANDS else 0))
                for i in range(2):
                    src = slice(i * C, i * C + C)
                    for odd in range(2):
                        o = tf[odd * C:odd * C + C, par, 2:RP + 2, i, 1 + 64 * half:65 + 64 * half]
                        a = proj_bank[src, :, odd::2, :].rearrange("c a r s -> c r a s")
                        x = xc[src, par, 1 + odd:1 + BAND:2, 1 + 64 * half:65 + 64 * half]
                        last = nc.vector.tensor_tensor(o.rearrange("c r (a s) -> c r a s", s=PATCH), a,
                                                       x.rearrange("c r (a s) -> c r a s", s=PATCH), ALU.add)
                last.then_inc(t_ready, 1)

            def transform(to, src, part, done, slots=RP):
                col = [src[:, 0:slots, :, c:c + W - 1:2] for c in range(4)]
                to = to[:, 0:slots]
                if part == 0:
                    nc.vector.tensor_tensor(to[:, :, 2], col[2], col[1], ALU.subtract)
                    nc.vector.tensor_tensor(to[:, :, 1], col[1], col[2], ALU.add).then_inc(done, 1)
                else:
                    nc.vector.tensor_tensor(to[:, :, 0], col[0], col[2], ALU.subtract)
                    nc.vector.tensor_tensor(to[:, :, 3], col[1], col[3], ALU.subtract).then_inc(done, 1)

            def t_inputs(G, b, par, part):
                if part == 0:
                    dve.wait_ge(t_ready, b * 2 + 2)
                    if G is not None:
                        dve.wait_ge(low_done[FROM1], splits_done(G, FROM1, 1))
                transform(d[FROM_T], tf[:, par, 2:RP + 2], part, d_done[FROM_T])

            def t_low(b, part):
                dve.wait_ge(high_done[FROM_T], b * 2 + (part + 1))
                streams = PARTS[part]
                nc.vector.tensor_tensor(dtl[:, 1:RP + 1, streams], d[FROM_T][:, :, streams],
                                        dth[:, 1:RP + 1, streams].bitcast(F32), ALU.subtract).then_inc(low_done[FROM_T], 1)

            def streams(which, k, n):
                lo, hi = pairs(which, k)
                bank = conv_bank[BANK[first_tile(which) + n]][:].rearrange("c (s i w) -> c s i w", i=2, w=WT)
                left, right = sums[which][:, lo:hi, :, 0::2], sums[which][:, lo:hi, :, 1::2]
                return bank[:, lo:hi], left, right, m2_sb[:, lo:hi]

            def middle(G, k, which):
                m1, left, right, m2 = streams(which, k, 1)
                dve.wait_ge(act_read, act_reads(G, 1 + which))
                dve.wait_ge(tile_done, tiles_done(G, first_tile(which) + 1))
                if which == CONV1 or G is ALL_STEPS:
                    dve.wait_ge(sent, G * 16 + 16)
                elif which != ODD:
                    dve.wait_ge(relu_done, sets_done(G, CONV1 if which == CONV3 else ODD))
                nc.vector.tensor_tensor(left, m1, m2, ALU.add).then_inc(sum_done, 1)
                nc.vector.tensor_tensor(right, m1, m2, ALU.subtract).then_inc(dve_read, 1)

            def add_m0(G, k, which):
                m0, left, _, _ = streams(which, k, 2)
                dve.wait_ge(tile_done, tiles_done(G, first_tile(which) + 2))
                dve.wait_ge(sum_done, sets_done(G, which))
                nc.vector.tensor_tensor(left, m0, left, ALU.add).then_inc(dve_read, 1)

            def less_m3(G, k, which, behind=0):
                m3, _, right, _ = streams(which, k, 3)
                dve.wait_ge(tile_done, tiles_done(G, first_tile(which) + (3 - behind * TILES)))
                dve.wait_ge(dve_read, dve_reads(G, 3 * which + (1 - behind * DVE_READS)))
                nc.vector.tensor_tensor(right, right, m3, ALU.subtract).then_inc(dve_read, 1)

            def inputs(G, k, b, n, part, behind=0):
                if part == 0:
                    if n == FROM1:
                        dve.wait_ge(low_done[FROM_EVEN], splits_done(G, FROM_EVEN, 1, 1))
                    elif n == FROM_ODD:
                        dve.wait_ge(low_done[FROM_ODD], splits_done(G, FROM_ODD, 1, 1 + behind))
                    else:
                        dve.wait_ge(low_done[FROM_T], b * 2)
                    which = {FROM1: CONV1, FROM_ODD: ODD, FROM_EVEN: EVEN}[n]
                    dve.wait_ge(relu_done, sets_done(G, which - behind * SETS))
                transform(d[n], relued, part, d_done[n], new_slots(n, k))

            def low(G, k, n, part, behind=0):
                dve.wait_ge(high_done[n], splits_done(G, n, part, behind))
                streams, at, slots = PARTS[part], new_slot[n], new_slots(n, k)
                high_part, low_part = (t[:, at:at + slots, streams] for t in (d_high[n], d_low[n]))
                nc.vector.tensor_tensor(low_part, d[n][:, 0:slots, streams], high_part.bitcast(F32),
                                        ALU.subtract).then_inc(low_done[n], 1)

            def finish(G, k, b):
                lo, hi = pairs3(k)
                dve.wait_ge(relu_done, sets_done(G, CONV3))
                dve.wait_ge(carried, b * 16 if k in (0, BANDS) else b * 16 - 16)
                o = sums[CONV3][:, lo:hi]
                nc.vector.tensor_tensor(o, o, tf[:, 1 - k % 2 if k else 0, lo:hi, :, 1:1 + W], ALU.add).then_inc(out_ready, 1)

            nc.vector.memset(rbd[:], 0.0)
            for c in (0, WP - 1):
                nc.vector.memset(relued[:, :, :, c:c + 1], 0.0)
                for i in range(2):
                    nc.vector.memset(tf[:, i, :, :, c:c + 1], 0.0)
            nc.vector.memset(tf[:, 0, 0:2, :, 1:1 + W], 0.0)
            nc.vector.memset(qk[:], 0.0).then_inc(zeroed, 1)
            dve.wait_ge(zeroed, 1)
            dve.wait_ge(qk_done, 1)
            nc.vector.tensor_copy(qk[0:C, 0:C], score_bank[0][0:C, 0:C])
            nc.vector.tensor_copy(qk[C:128, C:128], score_bank[0][C:128, 0:C]).then_inc(qk_ready, 1)

            max_scores(0, 0)
            max_scores(0, 1)
            norm(0, 0)
            norm(0, 1)
            dve.wait_ge(w_in, 48)
            split_weights(nc.vector, dve.wait_ge, raws[0], w1h, w1l, w_mid[:, :, 0:2], w_half[:, 0:2], w_stage, 0)
            max_scores(0, 2)
            norm(0, 2)
            max_scores(0, 3)
            norm(0, 3)
            add_x(None, 0, 0, 0, 0, 2)
            split_weights(nc.vector, dve.wait_ge, raws[1], w2h, w2l, w_mid, w_half, w_stage, 4).then_inc(split_done, 1)
            add_x(None, 0, 0, 0, 1, 3)
            dve.wait_ge(split_done, 2)
            for part in range(2):
                t_inputs(None, 0, 0, part)
            for part in range(2):
                t_low(0, part)

            def step(G, k, b, q, par, att):
                if k:
                    less_m3(G, k - 1, EVEN, 1)
                    inputs(G, k - 1, b, FROM_ODD, 0, 1)
                if att:
                    max_scores(b, 0)
                if k:
                    inputs(G, k - 1, b, FROM_ODD, 1, 1)
                if att:
                    max_scores(b, 1)
                    norm(b, 0)
                middle(G, k, CONV1)
                if att:
                    norm(b, 1)
                add_m0(G, k, CONV1)
                if k:
                    inputs(G, k - 1, b, FROM_EVEN, 0, 1)
                if k:
                    low(G, k - 1, FROM_ODD, 0, 1)
                if att:
                    max_scores(b, 2)
                if k:
                    low(G, k - 1, FROM_EVEN, 0, 1)
                less_m3(G, k, CONV1)
                if att:
                    norm(b, 2)
                    max_scores(b, 3)
                if k:
                    inputs(G, k - 1, b, FROM_EVEN, 1, 1)
                    low(G, k - 1, FROM_ODD, 1, 1)
                    low(G, k - 1, FROM_EVEN, 1, 1)
                if att:
                    norm(b, 3)
                inputs(G, k, b, FROM1, 0)
                middle(G, k, CONV3)
                inputs(G, k, b, FROM1, 1)
                low(G, k, FROM1, 0)
                add_m0(G, k, CONV3)
                low(G, k, FROM1, 1)
                less_m3(G, k, CONV3)
                finish(G, k, b)
                if att:
                    add_x(G, k, b, par, 0, b * 4 + 2)
                middle(G, k, ODD)
                add_m0(G, k, ODD)
                if att:
                    add_x(G, k, b, par, 1, b * 4 + 3)
                less_m3(G, k, ODD)
                if att:
                    t_inputs(G, b, par, 0)
                middle(G, k, EVEN)
                if att:
                    t_inputs(G, b, par, 1)
                    t_low(b, 0)
                add_m0(G, k, EVEN)
                if att:
                    t_low(b, 1)
                if k == BANDS:
                    less_m3(G, k, EVEN)
                    for n in (FROM_ODD, FROM_EVEN):
                        for part in range(2):
                            inputs(G, k, b + 1, n, part)
                        for part in range(2):
                            low(G, k, n, part)

            schedule(dve, step)
            middle(ALL_STEPS, 0, CONV3)
            add_m0(ALL_STEPS, 0, CONV3)
            less_m3(ALL_STEPS, 0, CONV3)
            finish(ALL_STEPS, 0, PAIRS * BANDS + 1)

        @block.gpsimd
        def _(pool):
            nc.gpsimd.memset(zeros[:], 0.0)
            for t in (*dvh, *dvl):
                nc.gpsimd.memset(t[:].bitcast(F32), 0.0)
            for i, (credit, n) in enumerate((
                    (act_read, ACT_READS), (dve_read, DVE_READS), (high_done[FROM_ODD], 2), (high_done[FROM_EVEN], 2),
                    (low_done[FROM_ODD], 2), (low_done[FROM_EVEN], 2), (sent, 16), (t_kept, 32), (u_kept, 32),
                    (carried, 16), (v_zeroed, 1))):
                nc.gpsimd.memset(credits[:, i:i + 1], 0.0).then_inc(credit, n)
            pool.wait_ge(w_in, 48)
            split_weights(nc.gpsimd, pool.wait_ge, raws[2], w3h, w3l, w3_mid, w3_half, w3_stage, 0).then_inc(split_done, 1)


def kernel(**inputs):
    import concourse.bacc as bacc
    from concourse.bass_utils import run_bass_kernel_spmd

    given = {n.removeprefix("L0_conv_"): np.asarray(a) for n, a in inputs.items()}
    f32 = np.float32

    padded = np.zeros((PAIRS, 2, H + 2, WP, C), f32)
    padded[:, :, 1:-1, 1:-1] = given["x"].reshape(2, PAIRS, H, W, C).swapaxes(0, 1)
    x_bands = np.zeros((LOADS, 128, HALO, WP), f32)
    x_keys = np.zeros((LOADS, HALO, HALO, PATCHES, 2, C), f32)
    for n in range(PAIRS * BANDS):
        p, row = n // BANDS, n % BANDS * BAND
        band = padded[p, :, row:row + HALO]
        x_bands[n] = band.transpose(0, 3, 1, 2).reshape(128, HALO, WP)
        for a in range(PATCHES):
            x_keys[n, :, :, a] = band[:, :, a * PATCH:a * PATCH + HALO].transpose(1, 2, 0, 3)

    vbd = np.zeros((128, 128), f32)
    vbd[:C, :C] = vbd[C:, C:] = given["V_P"]
    k1, k2, k3 = (given[f"ff{i}_kernel"] for i in (1, 2, 3))
    w1 = np.zeros((128, 2, 3, 128), f32)
    w2 = np.zeros((128, 4, 3, 128), f32)
    w3 = np.zeros((128, 4, 3, 128), f32)
    for c in range(3):
        for s in range(2):
            for i in range(2):
                for o in range(2):
                    tap = 2 * s + i - o
                    if 0 <= tap < 3:
                        w1[i * C:i * C + C, s, c, o * C:o * C + C] = k1[tap, c]
        for even in range(2):
            for s in range(2):
                for i in range(2):
                    tap = 2 * s + i - (0 if even else 1)
                    if 0 <= tap < 3:
                        w2[i * C:i * C + C, 2 * even + s, c] = k2[tap, c]
        for s in range(4):
            for o in range(2):
                if 0 <= s - o < 3:
                    w3[:, s, c, o * C:o * C + C] = k3[s - o, c]

    window = np.full((2, PATCH, PATCH, HALO, HALO), NEG, f32)
    for r in range(PATCH):
        for c in range(PATCH):
            window[:, r, c, r:r + 3, c:c + 3] = 0.0

    bf16 = mybir.dt.np(BF16)
    data = {
        "x_bands": x_bands,
        "x_keys": x_keys.reshape(LOADS, KEYS, PATCHES, 128),
        "qt2": np.concatenate([given["Q_P"].T, given["Q_P"].T], axis=1),
        "kt": given["K_P"].T,
        "vbd": vbd,
        "w1": w1,
        "w2": w2,
        "w3": w3,
        "b1": np.concatenate([given["ff1_bias"]] * 2).reshape(128, 1),
        "b2": given["ff2_bias"].reshape(128, 1),
        "b3": np.concatenate([given["ff3_bias"]] * 2).reshape(128, 1),
        "window": window.reshape(128, KEYS).astype(bf16),
        "eye": np.eye(128, dtype=f32),
        "eye16": np.eye(128, dtype=f32).astype(bf16),
    }
    nc = bacc.Bacc("TRN2", target_bir_lowering=False, num_devices=1)
    arrays, args = {}, []
    for name, a in data.items():
        arrays[name] = np.ascontiguousarray(a)
        args.append(nc.dram_tensor(name, a.shape, mybir.dt.from_np(a.dtype), kind="ExternalInput").ap())
    out = nc.dram_tensor("out", (128, ALL_STEPS + 1, RP, 2, W), F32, kind="ExternalOutput").ap()
    build(nc, *args, out)
    got = run_bass_kernel_spmd(nc, [arrays], core_ids=[0]).results[0]["out"]
    got = got[:, 1:].reshape(2, C, PAIRS, STEPS * RP, 2, W)[:, :, :, 2:2 + H // 2]
    return np.ascontiguousarray(got.transpose(4, 2, 3, 0, 5, 1)).reshape(IMAGES, H, W, C)
```
